# Optimizing a Trainium2 kernel written in Bass

```python
import numpy as np
import jax
import jax.numpy as jnp

def _softmax(x, axis=-1):
    return jax.nn.softmax(x, axis=axis)

def _gelu(x):
    return jax.nn.gelu(x, approximate=True)

def _silu(x):
    return jax.nn.silu(x)

def _sigmoid(x):
    return jax.nn.sigmoid(x)

def _layernorm(x, axis=-1, eps=1e-05):
    m = jnp.mean(x, axis=axis, keepdims=True)
    v = jnp.var(x, axis=axis, keepdims=True)
    return (x - m) / jnp.sqrt(v + eps)

def _scatter_add(tgt, idx, src, axis=0):
    return tgt.at[idx].add(src)

def _segment_sum(src, seg, n):
    return jax.ops.segment_sum(src, seg, n)
kernel_name = 'mk_adaln_d1_jaxref_r4_297c4b'

def setup_inputs(seed: int=0):
    np.random.seed(seed)
    _w = jnp.asarray

    def _L0_attn_setup():
        import jax, jax.numpy as jnp
        import numpy as np
        H = 256
        NH = 16
        HD = H // NH
        EPS = 1e-05

        def _attn_block(x, ln_gamma, ln_beta, W_qkv, b_qkv, W_out, b_out):
            B, S, _ = x.shape
            mu = jnp.mean(x, axis=-1, keepdims=True)
            var = jnp.mean(jnp.square(x - mu), axis=-1, keepdims=True)
            xn = (x - mu) / jnp.sqrt(var + EPS) * ln_gamma + ln_beta
            qkv = jnp.einsum('bsh,oh->bso', xn, W_qkv) + b_qkv
            qkv = qkv.reshape(B, S, 3, NH, HD).transpose(2, 0, 3, 1, 4)
            q, k, v = (qkv[0], qkv[1], qkv[2])
            scores = jnp.einsum('bhqd,bhkd->bhqk', q, k) / jnp.sqrt(jnp.asarray(HD, x.dtype))
            probs = jax.nn.softmax(scores, axis=-1)
            ctx = jnp.einsum('bhqk,bhkd->bhqd', probs, v)
            ctx = ctx.transpose(0, 2, 1, 3).reshape(B, S, H)
            out = jnp.einsum('bsh,oh->bso', ctx, W_out) + b_out
            return x + out
        key = jax.random.key(seed)
        ks = jax.random.split(key, 5)
        b_qkv = float(np.sqrt(6.0 / (H + 3 * H)))
        b_out = float(np.sqrt(6.0 / (H + H)))
        return {'hidden_states': jax.random.normal(ks[0], (2, 512, H), dtype=jnp.float32), 'ln_gamma': jnp.ones((H,), jnp.float32), 'ln_beta': jnp.zeros((H,), jnp.float32), 'W_qkv': jax.random.uniform(ks[1], (3 * H, H), jnp.float32, -b_qkv, b_qkv), 'b_qkv': jnp.zeros((3 * H,), jnp.float32), 'W_out': jax.random.uniform(ks[2], (H, H), jnp.float32, -b_out, b_out), 'b_out': jnp.zeros((H,), jnp.float32)}
    _L0_attn_in = _L0_attn_setup()

    def _L0_ffn_setup():
        import jax, jax.numpy as jnp
        import numpy as np
        B, S, D, O, E, K = (2, 512, 256, 256, 8, 2)
        key = jax.random.key(seed)
        ks = jax.random.split(key, 6)

        def w(k, shape, fan_in):
            return jax.random.normal(k, shape, jnp.float32) * fan_in ** (-0.5)
        return {'x': jax.random.normal(ks[0], (B, S, D), jnp.float32), 'gate_w': w(ks[1], (E, D), D), 'gate_b': jnp.zeros((E,), jnp.float32), 'w1': w(ks[2], (E, D, O), D), 'b1': jnp.zeros((E, O), jnp.float32), 'w2': w(ks[3], (E, O, O), O), 'b2': jnp.zeros((E, O), jnp.float32), 'w3': w(ks[4], (E, O, O), O), 'b3': jnp.zeros((E, O), jnp.float32)}
    _L0_ffn_in = _L0_ffn_setup()
    _L0_c = _w((lambda *s: np.random.randn(*s).astype(np.float32) * 0.05)(2, 256))
    _L0_wmod = _w((lambda *s: np.random.randn(*s).astype(np.float32) * 0.05)(256, 6 * 256) * 256 ** (-0.5))
    _d = {'L0_attn_hidden_states': _L0_attn_in['hidden_states'], 'L0_attn_ln_gamma': _L0_attn_in['ln_gamma'], 'L0_attn_ln_beta': _L0_attn_in['ln_beta'], 'L0_attn_W_qkv': _L0_attn_in['W_qkv'], 'L0_attn_b_qkv': _L0_attn_in['b_qkv'], 'L0_attn_W_out': _L0_attn_in['W_out'], 'L0_attn_b_out': _L0_attn_in['b_out'], 'L0_ffn_gate_w': _L0_ffn_in['gate_w'], 'L0_ffn_gate_b': _L0_ffn_in['gate_b'], 'L0_ffn_w1': _L0_ffn_in['w1'], 'L0_ffn_b1': _L0_ffn_in['b1'], 'L0_ffn_w2': _L0_ffn_in['w2'], 'L0_ffn_b2': _L0_ffn_in['b2'], 'L0_ffn_w3': _L0_ffn_in['w3'], 'L0_ffn_b3': _L0_ffn_in['b3'], 'L0_c': _L0_c, 'L0_wmod': _L0_wmod}
    _x0 = _d['L0_attn_hidden_states']
    _d['L0_attn_hidden_states'] = jax.random.normal(jax.random.fold_in(jax.random.key(seed), 1), (2, 2048, 256), dtype=_x0.dtype)
    del _x0
    return _d

def reference(L0_attn_hidden_states, L0_attn_ln_gamma, L0_attn_ln_beta, L0_attn_W_qkv, L0_attn_b_qkv, L0_attn_W_out, L0_attn_b_out, L0_ffn_gate_w, L0_ffn_gate_b, L0_ffn_w1, L0_ffn_b1, L0_ffn_w2, L0_ffn_b2, L0_ffn_w3, L0_ffn_b3, L0_c, L0_wmod):

    def _L0_attn_ref(hidden_states, ln_gamma, ln_beta, W_qkv, b_qkv, W_out, b_out):
        import jax, jax.numpy as jnp
        import numpy as np
        H = 256
        NH = 16
        HD = H // NH
        EPS = 1e-05

        def _attn_block(x, ln_gamma, ln_beta, W_qkv, b_qkv, W_out, b_out):
            B, S, _ = x.shape
            mu = jnp.mean(x, axis=-1, keepdims=True)
            var = jnp.mean(jnp.square(x - mu), axis=-1, keepdims=True)
            xn = (x - mu) / jnp.sqrt(var + EPS) * ln_gamma + ln_beta
            qkv = jnp.einsum('bsh,oh->bso', xn, W_qkv) + b_qkv
            qkv = qkv.reshape(B, S, 3, NH, HD).transpose(2, 0, 3, 1, 4)
            q, k, v = (qkv[0], qkv[1], qkv[2])
            scores = jnp.einsum('bhqd,bhkd->bhqk', q, k) / jnp.sqrt(jnp.asarray(HD, x.dtype))
            probs = jax.nn.softmax(scores, axis=-1)
            ctx = jnp.einsum('bhqk,bhkd->bhqd', probs, v)
            ctx = ctx.transpose(0, 2, 1, 3).reshape(B, S, H)
            out = jnp.einsum('bsh,oh->bso', ctx, W_out) + b_out
            return x + out
        return _attn_block(hidden_states, ln_gamma, ln_beta, W_qkv, b_qkv, W_out, b_out)

    def _L0_ffn_ref(x, gate_w, gate_b, w1, b1, w2, b2, w3, b3):
        import jax, jax.numpy as jnp
        import numpy as np
        B, S, D, O, E, K = (2, 512, 256, 256, 8, 2)
        probs = jax.nn.softmax(x @ gate_w.T + gate_b, axis=-1)
        _, topi = jax.lax.top_k(probs, K)
        onehot = jax.nn.one_hot(topi, E, dtype=probs.dtype)
        cw = jnp.einsum('bske,bsk->bse', onehot, probs[..., :K])
        out = jnp.zeros(x.shape[:2] + (O,), x.dtype)
        for e in range(E):
            h = jax.nn.relu(x @ w1[e] + b1[e])
            h = jax.nn.relu(h @ w2[e] + b2[e])
            h = h @ w3[e] + b3[e]
            out = out + cw[..., e:e + 1] * h
        return out
    x = L0_attn_hidden_states
    mod = (_silu(L0_c) @ L0_wmod).reshape(L0_c.shape[0], 6, 1, -1)
    sa, ca, ga, sb, cb, gb = (mod[:, 0], mod[:, 1], mod[:, 2], mod[:, 3], mod[:, 4], mod[:, 5])
    ga = (2 * (ga >= 0) - 1) * jnp.maximum(jnp.abs(ga), 0.25)
    gb = (2 * (gb >= 0) - 1) * jnp.maximum(jnp.abs(gb), 0.25)
    h = _layernorm(x, axis=-1) * (1 + ca) + sa
    x = x + ga * _L0_attn_ref(h, L0_attn_ln_gamma, L0_attn_ln_beta, L0_attn_W_qkv, L0_attn_b_qkv, L0_attn_W_out, L0_attn_b_out)
    h = _layernorm(x, axis=-1) * (1 + cb) + sb
    x = x + gb * _L0_ffn_ref(h, L0_ffn_gate_w, L0_ffn_gate_b, L0_ffn_w1, L0_ffn_b1, L0_ffn_w2, L0_ffn_b2, L0_ffn_w3, L0_ffn_b3)
    return x

_drawn_inputs = setup_inputs


def setup_inputs(seed=0):
    import zlib

    import numpy as np

    out = dict(_drawn_inputs(seed))
    spreads = {'L0_attn_ln_gamma': (1.0, 0.6),
     'L0_attn_ln_beta': (0.0, 0.413),
     'L0_attn_b_qkv': (0.0, 0.34),
     'L0_attn_b_out': (0.0, 0.34),
     'L0_ffn_gate_b': (0.0, 0.688),
     'L0_ffn_b1': (0.0, 2.0),
     'L0_ffn_b2': (0.0, 2.0),
     'L0_ffn_b3': (0.0, 0.8)}
    factors = {'L0_ffn_w1': 2.73}
    for name, (base, spread) in spreads.items():
        noise = np.random.default_rng([zlib.crc32(name.encode()), seed]).standard_normal(out[name].shape)
        drawn = base * np.exp(spread * noise) if base else spread * noise
        out[name] = jnp.asarray(drawn.astype(out[name].dtype))
    for name, factor in factors.items():
        out[name] = (out[name] * factor).astype(out[name].dtype)
    return out
```

```python
import concourse.bass as bass
from concourse import mybir
from contextlib import ExitStack

P = 128
B, S, H = 2, 2048, 256
HEADS, HD = 16, 16
EXPERTS = 8
EPS = 1e-5
FLOOR = 0.25
KC = H // P
CHUNK = 512
CHUNKS = S // CHUNK
TILES = CHUNK // P
STILES = S // P
HEADROWS = B * HEADS
PARTS = 3
TERMS = 6
TROWS = TERMS * HD
HEAD_DMAS = 2 * TERMS
VW = 32
C_COND, C_BQK, C_LNG, C_LNB = 0, 4, 8, 10
C_B1, C_B2 = 12, 28
C_IOTA, C_SEL = 44, 52
NCOLS = 52 + HD + 1
R_BV, R_BO, R_GB = 0, H, 2 * H
NROWS = 2 * H + EXPERTS
SA, CA, GA, SB_, CB, GB = range(6)
M_CA, M_SA, M_GA, M_GB = range(4)


def build(nc, x, cols, rows, wmod, wqkv_t, wout_t, gate_t, w1, w2, w3, b3, ident, ident_b, out):
    f32, bf16, u32 = mybir.dt.float32, mybir.dt.bfloat16, mybir.dt.uint32
    ALU, ACT, AX = mybir.AluOpType, mybir.ActivationFunctionType, mybir.AxisListType
    ds = bass.ds
    ctx = ExitStack()

    def sb(name, shape, dt=f32):
        return ctx.enter_context(nc.sbuf_tensor(name, shape, dt))

    def sem(name):
        return ctx.enter_context(nc.semaphore(name))

    with ctx:
        q_parts = nc.dram_tensor("q_parts", [PARTS, HEADROWS * HD, S], bf16, kind="Internal").ap()
        k_parts = nc.dram_tensor("k_parts", [PARTS, HEADROWS * HD, S], bf16, kind="Internal").ap()

        xs = sb("xs", [P, B, STILES, H])
        cs = sb("cs", [P, NCOLS])
        rs = sb("rs", [P, NROWS])
        mod = sb("mod", [P, B, 4, H])
        gabo = sb("gabo", [P, B, H])
        modc = sb("modc", [P, 2, KC, B])
        wqkv = sb("wqkv", [P, KC, 3 * H])
        wout = sb("wout", [P, KC, H])
        gatew = sb("gatew", [P, KC, EXPERTS])
        b3s = sb("b3s", [EXPERTS, H])
        idf = sb("idf", [P, P])
        idb = sb("idb", [P, P], bf16)
        cw = sb("cw", [P, B, STILES, EXPERTS])
        small = sb("small", [P, 512])
        vall = sb("vall", [P, HEADROWS * STILES * HD])
        call = sb("call", [P, HEADROWS * STILES * HD])
        pall = sb("pall", [P, STILES * CHUNK])
        wreg = sb("wreg", [P, KC * 6 * H])
        q6 = sb("q6", [P, 2, S], bf16)
        k6 = sb("k6", [P, 2, S], bf16)
        vs = sb("vs", [P, 2, STILES, VW])
        acc_sb = sb("acc_sb", [P, 2, CHUNK])
        t3 = sb("t3", [P, 4 * TILES * H])

        v_heads = vall[:, :].rearrange("p (g t d) -> p g t d", t=STILES, d=HD)
        h_t = vall[:, :].rearrange("p (k b s) -> p k b s", k=KC, b=B)
        ctx_q = call[:, :].rearrange("p (n d) -> p n d", d=HD)
        ctx_h = call[:, :].rearrange("p (b h t d) -> p b h t d", b=B, h=HEADS, d=HD)
        s1 = call[:, :].rearrange("p (u b n) -> p u b n", u=4, b=B)
        h_tile = s1[:, 0].rearrange("p b (t f) -> p b t f", f=H)
        y_tile = s1[:, 1].rearrange("p b (t f) -> p b t f", f=H)
        xn_t = s1[:, 2].rearrange("p b (k s) -> p b k s", k=KC)
        xr_tile = s1[:, 3].rearrange("p b (t f) -> p b t f", f=H)
        qk_f = pall[:, 0:4 * CHUNK].rearrange("p (o s) -> p o s", o=4)
        parts = pall[:, 4 * CHUNK:].bitcast(bf16).rearrange("p (b o r s) -> p b o r s", b=B, o=4, r=PARTS)
        rest = acc_sb
        prob = pall[:, :].rearrange("p (k s) -> p k s", s=CHUNK)
        acc = pall[:, :].rearrange("p (b t f) -> p b t f", b=B, f=H)
        wm = wreg[:, :].rearrange("p (k n) -> p k n", k=KC)
        wx = wreg[:, :].rearrange("p (s l k n) -> p s l k n", s=2, l=3, k=KC)
        hid = call[:, 0:8 * CHUNK].rearrange("p (l b k s) -> p l b k s", l=2, b=B, k=KC)
        o_tile = call[:, 8 * CHUNK:12 * CHUNK].rearrange("p (b t f) -> p b t f", b=B, f=H)
        t3v = t3[:, :].rearrange("p (u n) -> p u n", u=4)
        c_tile = [t3v[:, b].rearrange("p (t f) -> p t f", f=H) for b in range(B)]
        z_tile = [t3v[:, 2 + b].rearrange("p (t f) -> p t f", f=H) for b in range(B)]
        ctx_t = [acc_sb[:, :, :], vs[:, :, :, :].rearrange("p a t w -> p a (t w)")]
        hc_t = [r[:, 0, :].bitcast(f32).rearrange("p (k s) -> p k s", k=KC) for r in (q6, k6)]

        at = [0]

        def piece(n):
            at[0] += n
            return small[:, at[0] - n:at[0]]

        stats = [piece(TILES * 6).rearrange("p (t n) -> p t n", n=6) for _ in range(B)]
        mv = [piece(TILES * 2).rearrange("p (t n) -> p t n", n=2) for _ in range(B)]
        rstd = [piece(TILES) for _ in range(B)]
        var = [piece(TILES) for _ in range(B)]
        std = [piece(TILES) for _ in range(B)]
        mx = [piece(8).rearrange("p (t n) -> p t n", n=2) for _ in range(2)]
        silu = piece(4)
        mtop = [piece(4) for _ in range(2)]
        mneg = piece(4)
        mres = piece(4)
        mres2 = piece(4)
        sig = piece(4)
        free_at_first = piece(2)
        gl = [piece(32).rearrange("p (t e) -> p t e", e=EXPERTS) for _ in range(B)]
        gp = [piece(32).rearrange("p (t e) -> p t e", e=EXPERTS) for _ in range(B)]
        gtop = [piece(32).rearrange("p (t e) -> p t e", e=8) for _ in range(B)]
        gcw = [piece(32).rearrange("p (t e) -> p t e", e=EXPERTS) for _ in range(B)]
        g1 = [piece(4) for _ in range(B)]
        rec = [piece(4) for _ in range(B)]
        gidx = [sb(f"gidx{b}", [P, TILES, 8], u32) for b in range(B)]
        gidf = [sb(f"gidf{b}", [P, TILES, 8]) for b in range(B)]
        mparts = [sb(f"mparts{n}", [P, PARTS, TILES], bf16) for n in range(2)]
        mrows = [sb(f"mrows{n}", [PARTS * TILES, P], bf16) for n in range(2)]
        cond_b = t3v[:, 0, 0:KC * B * P].rearrange("p (k b n) -> p k b n", k=KC, b=B)
        gtmp = t3v[:, 1, 0:2 * H].rearrange("p (a n) -> p a n", a=2)
        cwt = [wqkv[0:EXPERTS, b, 0:CHUNK] for b in range(B)]

        ps = ctx.enter_context(nc.psum_tensor("ps", [P, 8, CHUNK], f32))
        MISC, ACC, ST = 7, 6, 4
        acc_ps = ps[:, ACC, :]
        ctx_ps = ps[:, MISC, 0:TILES * (HD + 1)].rearrange("p (t n) -> p t n", t=TILES)
        mt_ps = ps[0:PARTS * TILES, MISC, 0:P // 2].bitcast(bf16)
        sel = cs[:, C_SEL:C_SEL + HD + 1]

        cols_in = sem("cols_in")
        const_in = sem("const_in")
        x_in = sem("x_in")
        wmod_in = sem("wmod_in")
        sig_done = sem("sig_done")
        cond_done = sem("cond_done")
        mod_mm = sem("mod_mm")
        mod_done = sem("mod_done")
        fixed_done = sem("fixed_done")
        dve_step = sem("dve_step")
        pool_step = sem("pool_step")
        var_ready = sem("var_ready")
        std_ready = sem("std_ready")
        ln1_done = sem("ln1_done")
        h_ready = sem("h_ready")
        xr_done = sem("xr_done")
        y_ready = sem("y_ready")
        xt_mm = sem("xt_mm")
        xn_ready = sem("xn_ready")
        qk_mm = sem("qk_mm")
        v_mm = sem("v_mm")
        part1_ready = sem("part1_ready")
        parts_ready = sem("parts_ready")
        v_ready = sem("v_ready")
        parts_out = [sem(f"parts_out{b}") for b in range(B)]
        head_in = [sem(f"head_in{s}") for s in range(2)]
        v_staged = sem("v_staged")
        scores_mm = sem("scores_mm")
        max_done = sem("max_done")
        top_done = sem("top_done")
        m_parts = sem("m_parts")
        mt_mm = sem("mt_mm")
        mt_copied = sem("mt_copied")
        m_in = [sem(f"m_in{s}") for s in range(2)]
        st_mm = sem("st_mm")
        exp_done = sem("exp_done")
        pv_mm = sem("pv_mm")
        acc_out = sem("acc_out")
        ctx_mm = sem("ctx_mm")
        ctx_done = sem("ctx_done")
        c_copied = sem("c_copied")
        ct_mm = sem("ct_mm")
        ct_ready = sem("ct_ready")
        proj_mm = sem("proj_mm")
        proj_read = sem("proj_read")
        z_ready = sem("z_ready")
        ht_mm = sem("ht_mm")
        ht_ready = sem("ht_ready")
        gate_mm = sem("gate_mm")
        gl_ready = sem("gl_ready")
        ge_ready = sem("ge_ready")
        cw_ready = sem("cw_ready")
        cwt_mm = sem("cwt_mm")
        cwt_ready = sem("cwt_ready")
        b3_mm = sem("b3_mm")
        acc_init = sem("acc_init")
        w_in = [sem(f"w_in{s}") for s in range(2)]
        l1_mm = sem("l1_mm")
        l1_out = sem("l1_out")
        l2_mm = sem("l2_mm")
        l2_out = sem("l2_out")
        l3_mm = sem("l3_mm")
        l3_out = sem("l3_out")
        o_ready = sem("o_ready")
        o_out = [sem(f"o_out{b}") for b in range(B)]

        CONSTS = 7 * 16
        STEPS = HEADROWS * CHUNKS
        QUADS = STILES // 4
        OPS = 2 * TILES
        FLAT = EXPERTS * CHUNKS

        def wait_apart(eng, semaphore, value):
            eng.wait_ge(semaphore, value)
            eng.nop(nofuse=True)

        def on_two(ap, n):
            return ap.unsqueeze(1).to_broadcast([P, n, ap.shape[1]])

        block = ctx.enter_context(nc.Block())

        @block.sync
        def _(sp):
            sp.dma_start(cs[:, :], cols).then_inc(cols_in, 16)
            sp.dma_start(wm, wmod.rearrange("(k p) n -> p k n", p=P)).then_inc(wmod_in, 16)
            xv = x.rearrange("b (t p) f -> p b t f", p=P)
            for c in range(CHUNKS):
                for b in range(B):
                    t = ds(c * TILES, TILES)
                    sp.dma_start(xs[:, b, t, :], xv[:, b, t, :]).then_inc(x_in, 16)
            sp.dma_start(rs[:, :], rows).then_inc(const_in, 16)
            sp.dma_start(wqkv[:, :, :], wqkv_t.rearrange("(k p) n -> p k n", p=P)).then_inc(const_in, 16)
            sp.dma_start(wout[:, :, :], wout_t.rearrange("(k p) n -> p k n", p=P)).then_inc(const_in, 16)
            sp.dma_start(gatew[:, :, :], gate_t.rearrange("(k p) n -> p k n", p=P)).then_inc(const_in, 16)
            sp.dma_start(b3s[:, :], b3).then_inc(const_in, 16)
            sp.dma_start(idf[:, :], ident).then_inc(const_in, 16)
            sp.dma_start(idb[:, :], ident_b).then_inc(const_in, 16)

            with sp.Fori(0, CHUNKS) as c:
                for b in range(B):
                    sp.wait_ge(parts_ready, c * (4 * B) + 4 * (b + 1))
                    for o in range(4):
                        row = (b * KC + o % KC) * P
                        dst = (q_parts, k_parts)[o // KC][:, row:row + P, ds(c * CHUNK, CHUNK)]
                        sp.dma_start(dst.rearrange("r p s -> p r s"), parts[:, b, o]).then_inc(parts_out[b], 16)

            def load_head(g, s):
                for term, (qr, kr) in enumerate(((0, 0), (0, 1), (0, 2), (1, 0), (1, 1), (2, 0))):
                    for dst, src, r in ((q6, q_parts, qr), (k6, k_parts, kr)):
                        sp.dma_start(dst[term * HD:(term + 1) * HD, s, :],
                                     src[r, ds(g * HD, HD), :]).then_inc(head_in[s], 16)

            def load_m(n, par, s, c):
                sp.wait_ge(mt_copied, n + 1)
                for r in range(PARTS):
                    sp.dma_start(q6[TROWS + r:TROWS + r + 1, s, c * CHUNK:(c + 1) * CHUNK],
                                 mrows[par][r * TILES:(r + 1) * TILES, :]).then_inc(m_in[par], 16)

            for b in range(B):
                sp.wait_ge(parts_out[b], 16 * 4 * CHUNKS)
            load_head(0, 0)
            load_m(0, 0, 0, 0)

            def steps(i, first, last):
                for s in range(2):
                    if not (last and s == 1):
                        if not (first and s == 0):
                            sp.wait_ge(st_mm, (i * 2 + s) * (CHUNKS * STILES))
                        load_head(i * 2 + (s + 1), 1 - s)
                    for c in range(CHUNKS):
                        if last and s == 1 and c == CHUNKS - 1:
                            continue
                        n = i * (2 * CHUNKS) + (s * CHUNKS + c)
                        load_m(n + 1, (c + 1) % 2, (s + (c + 1) // CHUNKS) % 2, (c + 1) % CHUNKS)

            steps(0, True, False)
            with sp.Fori(1, HEADROWS // 2 - 1) as i:
                steps(i, False, False)
            steps(HEADROWS // 2 - 1, False, True)

            def load_weights(e, s):
                for l, w in enumerate((w1, w2, w3)):
                    sp.dma_start(wx[:, s, l], w[e].rearrange("(k p) n -> p k n", p=P)).then_inc(w_in[s], 16)

            for s in range(2):
                load_weights(s, s)
            with sp.Fori(1, EXPERTS // 2) as e2:
                for s in range(2):
                    sp.wait_ge(l3_mm, (e2 * 2 + (s - 1)) * (4 * CHUNKS))
                    load_weights(e2 * 2 + s, s)
            ov = out.rearrange("b (t p) f -> p b t f", p=P)
            with sp.Fori(0, CHUNKS) as c:
                for b in range(B):
                    sp.wait_ge(o_ready, c * B + (b + 1))
                    sp.dma_start(ov[:, b, ds(c * TILES, TILES), :], o_tile[:, b]).then_inc(o_out[b], 16)
            for b in range(B):
                sp.wait_ge(o_out[b], 16 * CHUNKS)

        @block.tensor
        def _(pe):
            mm = nc.tensor.matmul
            pe.wait_ge(cond_done, 2)
            pe.wait_ge(wmod_in, 16)
            for b in range(B):
                for n in range(3):
                    for k in range(KC):
                        last = mm(ps[:, 3 * b + n, :], cond_b[:, k, b, :], wm[:, k, n * CHUNK:(n + 1) * CHUNK],
                                  start=(k == 0), stop=(k == KC - 1))
            for kind, blk in enumerate((SB_, CB)):
                for f in range(KC):
                    for k in range(KC):
                        col = (kind * KC + f) * B
                        last = mm(ps[:, 6, col:col + B], wm[:, k, blk * H + f * P:blk * H + (f + 1) * P],
                                  cond_b[:, k, :, 0], start=(k == 0), stop=(k == KC - 1))
            last.then_inc(mod_mm, 1)

            pe.wait_ge(const_in, CONSTS)
            pe.wait_ge(mod_done, 1)
            with pe.Fori(0, CHUNKS) as c:
                for b in range(B):
                    pe.wait_ge(y_ready, c * B + (b + 1))
                    if b:
                        pe.wait_ge(xn_ready, c * (2 * B) + 2 * b)
                    for k in range(KC):
                        for t in range(TILES):
                            last = nc.tensor.transpose(ps[:, k, t * P:(t + 1) * P],
                                                       y_tile[:, b, t, k * P:(k + 1) * P], idf[:, :])
                    last.then_inc(xt_mm, 1)
                for b in range(B):
                    pe.wait_ge(xn_ready, c * (2 * B) + 2 * (b + 1))
                    for o in range(4):
                        if b:
                            pe.wait_ge(part1_ready, c * (4 * B) + (o + 1))
                        for k in range(KC):
                            last = mm(ps[:, 2 + o, :], wqkv[:, k, o * P:(o + 1) * P], xn_t[:, b, k, :],
                                      start=(k == 0), stop=(k == KC - 1))
                        last.then_inc(qk_mm, 1)
                    for u in range(2):
                        if b:
                            pe.wait_ge(v_ready, c * (2 * B) + (u + 1))
                        for t in (2 * u, 2 * u + 1):
                            for k in range(KC):
                                last = mm(ps[:, 6 + u, (t % 2) * H:(t % 2 + 1) * H],
                                          xn_t[:, b, k, t * P:(t + 1) * P], wqkv[:, k, 2 * H:3 * H],
                                          start=(k == 0), stop=(k == KC - 1))
                        last.then_inc(v_mm, 1)

            def scores(n, s, c, u):
                t, kb = u // 4, u % 4
                if u % 2 == 0 and not (isinstance(n, int) and 2 * OPS * n + u < 4):
                    pe.wait_ge(max_done, n * OPS + (u // 2 - 1))
                q0 = c * CHUNK + t * P
                last = mm(ps[:, (u % 4), :], q6[0:TROWS, s, q0:q0 + P],
                          k6[0:TROWS, s, kb * CHUNK:(kb + 1) * CHUNK], start=True, stop=True)
                if u % 2:
                    last.then_inc(scores_mm, 1)

            def m_transpose(n, par):
                pe.wait_ge(m_parts, n + 1)
                nc.tensor.transpose(mt_ps, mparts[par][:, :, :].rearrange("p r t -> p (r t)"),
                                    idb[:, :]).then_inc(mt_mm, 1)

            def pv(n, s, q):
                pe.wait_ge(exp_done, n * STILES + 4 * (q + 1))
                if q == 0 and not (isinstance(n, int) and n == 0):
                    pe.wait_ge(acc_out, n)
                for j in range(4):
                    k = 4 * q + j
                    last = mm(ps[32 * j:32 * (j + 1), ACC, :], vs[:, s, k, :], prob[:, k, :],
                              start=(q == 0), stop=(q == QUADS - 1))
                last.then_inc(pv_mm, 1)

            def ctx_out(n, par):
                pe.wait_ge(acc_out, n + 1)
                for t in range(TILES):
                    last = mm(ctx_ps[:, t, :], acc_sb[:, par, t * P:(t + 1) * P], sel, start=True, stop=True)
                last.then_inc(ctx_mm, 1)

            def steps(i, first, last):
                for s in range(2):
                    for c in range(CHUNKS):
                        n = i * (2 * CHUNKS) + (s * CHUNKS + c)
                        step0 = first and s == 0 and c == 0
                        c2, s2 = (c + 2) % CHUNKS, (s + (c + 2) // CHUNKS) % 2
                        ahead = not (last and s == 1 and c >= 2)
                        if c == 0:
                            pe.wait_ge(v_staged, i * 2 + (s + 1))
                        if c == 2 and ahead:
                            pe.wait_ge(head_in[s2], (i + (s + 1) // 2 + 1) * (HEAD_DMAS * 16))
                        pe.wait_ge(m_in[c % 2], (i * CHUNKS + (s * CHUNKS + c) // 2 + 1) * (PARTS * 16))
                        for q in range(QUADS):
                            for j in range(4):
                                k = 4 * q + j
                                if not (step0 and k < 2):
                                    pe.wait_ge(exp_done, n * STILES + (k - 1))
                                mm(ps[:, ST + k % 2, :], k6[0:TROWS + PARTS, s, k * P:(k + 1) * P],
                                   q6[0:TROWS + PARTS, s, c * CHUNK:(c + 1) * CHUNK],
                                   start=True, stop=True).then_inc(st_mm, 1)
                                if ahead:
                                    scores(n + 2, s2, c2, k)
                            if q == 0:
                                if not step0:
                                    pv(n - 1, (s + (c - 1) // CHUNKS) % 2, QUADS - 1)
                            else:
                                pv(n, s, q - 1)
                            if q == 1 and not (last and s == 1 and c == CHUNKS - 1):
                                if not (first and s == 0 and c < 2):
                                    pe.wait_ge(ctx_done, n - 1)
                                m_transpose(n + 1, (c + 1) % 2)
                            if q == QUADS - 1 and not step0:
                                if not (last and s == 1 and c == CHUNKS - 1):
                                    pe.wait_ge(mt_copied, n + 2)
                                else:
                                    pe.wait_ge(ctx_done, n - 1)
                                ctx_out(n - 1, (c + 1) % 2)

            pe.wait_ge(fixed_done, 1)
            pe.wait_ge(head_in[0], HEAD_DMAS * 16)
            pe.wait_ge(v_ready, 2 * B * CHUNKS)
            pe.wait_ge(part1_ready, 4 * B * CHUNKS)
            for n in range(2):
                for u in range(STILES):
                    scores(n, 0, n, u)
            m_transpose(0, 0)
            pe.wait_ge(mt_copied, 1)
            steps(0, True, False)
            with pe.Fori(1, HEADROWS // 2 - 1) as i:
                steps(i, False, False)
            steps(HEADROWS // 2 - 1, False, True)
            pv(STEPS - 1, 1, QUADS - 1)
            pe.wait_ge(ctx_done, STEPS - 1)
            ctx_out(STEPS - 1, 1)

            with pe.Fori(0, CHUNKS) as c:
                for b in range(B):
                    pe.wait_ge(c_copied, c * B + (b + 1))
                    if b:
                        pe.wait_ge(ct_ready, c * (2 * B) + 2 * b)
                    for k in range(KC):
                        for t in range(TILES):
                            last = nc.tensor.transpose(ps[:, k, t * P:(t + 1) * P],
                                                       c_tile[b][:, t, k * P:(k + 1) * P], idf[:, :])
                    last.then_inc(ct_mm, 1)
                for b in range(B):
                    pe.wait_ge(ct_ready, c * (2 * B) + 2 * (b + 1))
                    if b:
                        pe.wait_ge(proj_read, c * B + b)
                    for t in range(TILES):
                        for k in range(KC):
                            last = mm(ps[:, 2 + t // 2, (t % 2) * H:(t % 2 + 1) * H],
                                      ctx_t[b][:, k, t * P:(t + 1) * P], wout[:, k, :],
                                      start=(k == 0), stop=(k == KC - 1))
                    last.then_inc(proj_mm, 1)
                for b in range(B):
                    pe.wait_ge(z_ready, c * B + (b + 1))
                    if b:
                        pe.wait_ge(ht_ready, c * (2 * B) + 2 * b)
                    for k in range(KC):
                        for t in range(TILES):
                            last = nc.tensor.transpose(ps[:, 4 + k, t * P:(t + 1) * P],
                                                       z_tile[b][:, t, k * P:(k + 1) * P], idf[:, :])
                    last.then_inc(ht_mm, 1)
                for b in range(B):
                    pe.wait_ge(ht_ready, c * (2 * B) + 2 * (b + 1))
                    if b:
                        pe.wait_ge(gl_ready, c * B + b)
                    for t in range(TILES):
                        for k in range(KC):
                            last = mm(ps[:, 6, t * EXPERTS:(t + 1) * EXPERTS],
                                      hc_t[b][:, k, t * P:(t + 1) * P], gatew[:, k, :],
                                      start=(k == 0), stop=(k == KC - 1))
                    last.then_inc(gate_mm, 1)
                for b in range(B):
                    pe.wait_ge(cw_ready, c * B + (b + 1))
                    if b:
                        pe.wait_ge(cwt_ready, c * B + b)
                    for t in range(TILES):
                        last = nc.tensor.transpose(ps[0:EXPERTS, 7, t * P:(t + 1) * P], gcw[b][:, t, :], idf[:, :])
                    last.then_inc(cwt_mm, 1)
                    pe.wait_ge(cwt_ready, c * B + (b + 1))
                    if b:
                        pe.wait_ge(acc_init, c * B + b)
                    for t in range(TILES):
                        last = mm(ps[:, 2 + t // 2, (t % 2) * H:(t % 2 + 1) * H],
                                  cwt[b][:, t * P:(t + 1) * P], b3s[:, :], start=True, stop=True)
                    last.then_inc(b3_mm, 1)

            with pe.Fori(0, EXPERTS // 2) as e2:
                for s in range(2):
                    wait_apart(pe, w_in[s], (e2 + 1) * (3 * 16))
                    with pe.Fori(0, CHUNKS) as c:
                        f4 = e2 * (8 * CHUNKS) + c * 4 + s * (4 * CHUNKS)
                        for b in range(B):
                            for fo in range(KC):
                                pe.wait_ge(l2_out, f4 + (2 * b + fo + 1))
                                for k in range(KC):
                                    last = mm(ps[:, 2 * b + fo, :], wx[:, s, 0, k, fo * P:(fo + 1) * P],
                                              h_t[:, k, b, ds(c * CHUNK, CHUNK)],
                                              start=(k == 0), stop=(k == KC - 1))
                                last.then_inc(l1_mm, 1)
                        for b in range(B):
                            pe.wait_ge(l1_out, f4 + 2 * (b + 1))
                            for fo in range(KC):
                                for k in range(KC):
                                    last = mm(ps[:, 2 * b + fo, :], wx[:, s, 1, k, fo * P:(fo + 1) * P],
                                              hid[:, 0, b, k, :], start=(k == 0), stop=(k == KC - 1))
                                last.then_inc(l2_mm, 1)
                        for b in range(B):
                            pe.wait_ge(l2_out, f4 + (4 + 2 * (b + 1)))
                            for u in range(2):
                                pe.wait_ge(l3_out, f4 + (2 * b + u + 1))
                                for t in (2 * u, 2 * u + 1):
                                    for k in range(KC):
                                        last = mm(ps[:, 4 + 2 * b + u, (t % 2) * H:(t % 2 + 1) * H],
                                                  hid[:, 1, b, k, t * P:(t + 1) * P], wx[:, s, 2, k, :],
                                                  start=(k == 0), stop=(k == KC - 1))
                                last.then_inc(l3_mm, 1)

        @block.scalar
        def _(act):
            act.wait_ge(cols_in, 16)
            nc.scalar.activation(sig, cs[:, C_COND:C_COND + 4], ACT.Exp, scale=-1.0).then_inc(sig_done, 1)
            act.wait_ge(const_in, CONSTS)

            with act.Fori(0, CHUNKS) as c:
                for n in range(2 * B):
                    act.wait_ge(var_ready, c * (2 * B) + (n + 1))
                    nc.scalar.activation(std[n % B], var[n % B], ACT.Sqrt).then_inc(std_ready, 1)
                for b in range(B):
                    act.wait_ge(xt_mm, c * B + (b + 1))
                    for k in range(KC):
                        nc.scalar.activation(xn_t[:, b, k, :], ps[:, k, :], ACT.Identity,
                                             scale=cs[:, C_LNG + k:C_LNG + k + 1],
                                             bias=cs[:, C_LNB + k:C_LNB + k + 1]).then_inc(xn_ready, 1)
                for b in range(B):
                    for o in range(4):
                        act.wait_ge(qk_mm, c * (4 * B) + (4 * b + o + 1))
                        if b:
                            act.wait_ge(parts_ready, c * (4 * B) + (o + 1))
                        bias = cs[:, C_BQK + o:C_BQK + o + 1]
                        nc.scalar.activation(qk_f[:, o, :], ps[:, 2 + o, :], ACT.Identity, bias=bias)
                        nc.scalar.activation(parts[:, b, o, 0, :], ps[:, 2 + o, :], ACT.Identity,
                                             bias=bias).then_inc(part1_ready, 1)

            def acc_copy(n, par):
                act.wait_ge(pv_mm, (n + 1) * QUADS)
                nc.scalar.activation(acc_sb[:, par, :], acc_ps, ACT.Copy).then_inc(acc_out, 1)

            def steps(i, first, last):
                for s in range(2):
                    for c in range(CHUNKS):
                        n = i * (2 * CHUNKS) + (s * CHUNKS + c)
                        step0 = first and s == 0 and c == 0
                        for k in range(STILES):
                            if k % 4 == 0 and not step0:
                                act.wait_ge(pv_mm, (n - 1) * QUADS + (k // 4 + 1))
                            act.wait_ge(st_mm, n * STILES + (k + 1))
                            nc.scalar.activation(prob[:, k, :], ps[:, ST + k % 2, :], ACT.Exp,
                                                 scale=HD ** -0.5).then_inc(exp_done, 1)
                            if k == 4 and not step0:
                                if not (first and s == 0 and c < 3):
                                    act.wait_ge(ctx_mm, n - 2)
                                acc_copy(n - 1, (c + 1) % 2)

            for b in range(B):
                act.wait_ge(parts_out[b], 16 * 4 * CHUNKS)
            steps(0, True, False)
            with act.Fori(1, HEADROWS // 2 - 1) as i:
                steps(i, False, False)
            steps(HEADROWS // 2 - 1, False, True)
            act.wait_ge(ctx_mm, STEPS - 2)
            acc_copy(STEPS - 1, 1)

            act.wait_ge(ctx_done, STEPS)
            with act.Fori(0, CHUNKS) as c:
                for b in range(B):
                    nc.scalar.activation(c_tile[b].rearrange("p t (h d) -> p h t d", d=HD),
                                         ctx_h[:, b, :, ds(c * TILES, TILES), :], ACT.Copy).then_inc(c_copied, 1)
                for b in range(B):
                    act.wait_ge(ct_mm, c * B + (b + 1))
                    for k in range(KC):
                        nc.scalar.activation(ctx_t[b][:, k, :], ps[:, k, :], ACT.Copy).then_inc(ct_ready, 1)
                for b in range(B):
                    act.wait_ge(var_ready, c * B + (2 * B * CHUNKS + b + 1))
                    nc.scalar.activation(std[b], var[b], ACT.Sqrt).then_inc(std_ready, 1)
                for b in range(B):
                    wait_apart(act, ht_mm, c * B + (b + 1))
                    for k in range(KC):
                        args = dict(bias=modc[:, 0, k, b:b + 1], scale=modc[:, 1, k, b:b + 1])
                        nc.scalar.activation(h_t[:, k, b, ds(c * CHUNK, CHUNK)], ps[:, 4 + k, :],
                                             ACT.Identity, **args)
                        nc.scalar.activation(hc_t[b][:, k, :], ps[:, 4 + k, :], ACT.Identity,
                                             **args).then_inc(ht_ready, 1)
                for b in range(B):
                    act.wait_ge(gl_ready, c * B + (b + 1))
                    nc.scalar.activation(gp[b], gl[b], ACT.Exp).then_inc(ge_ready, 1)
                for b in range(B):
                    wait_apart(act, b3_mm, c * B + (b + 1))
                    nc.scalar.activation(acc[:, b, ds(c * TILES, TILES), :].rearrange("p t f -> p (t f)"),
                                         ps[:, 2:4, :].rearrange("p a n -> p (a n)"),
                                         ACT.Copy).then_inc(acc_init, 1)

            act.wait_ge(ct_mm, B * CHUNKS)
            with act.Fori(0, EXPERTS // 2) as e2:
                for s in range(2):
                    with act.Fori(0, CHUNKS) as c:
                        f4 = e2 * (8 * CHUNKS) + c * 4 + s * (4 * CHUNKS)
                        for b in range(B):
                            for fo in range(KC):
                                wait_apart(act, l1_mm, f4 + (2 * b + fo + 1))
                                nc.scalar.activation(
                                    hid[:, 0, b, fo, :], ps[:, 2 * b + fo, :], ACT.Relu,
                                    bias=cs[:, ds(e2 * (2 * KC) + (C_B1 + s * KC + fo), 1)]).then_inc(l1_out, 1)

        @block.vector
        def _(dve):
            v = nc.vector
            count = [0]

            def step(ins):
                ins.then_inc(dve_step, 1)
                count[0] += 1
                dve.wait_ge(dve_step, count[0])

            v.memset(vs[:, :, :, :], 0.0).then_inc(dve_step, 1)
            v.memset(k6[96:128, :, :], 1.0)
            dve.wait_ge(dve_step, 1)
            count[0] = 1
            v.memset(vs[:, :, :, HD:HD + 1], 1.0).then_inc(fixed_done, 1)
            dve.wait_ge(sig_done, 1)
            dve.wait_ge(cols_in, 16)
            step(v.tensor_scalar(mneg, sig, 1.0, None, ALU.add))
            step(v.reciprocal(mres, mneg))
            step(v.tensor_tensor(silu, mres, cs[:, C_COND:C_COND + 4], ALU.mult))
            for k in range(KC):
                v.tensor_copy(cond_b[:, k], silu[:, k * B:(k + 1) * B].unsqueeze(2).to_broadcast([P, B, P])
                              ).then_inc(cond_done, 1)
            dve.wait_ge(mod_mm, 1)
            dve.wait_ge(const_in, CONSTS)
            for b in range(B):
                def blk(i):
                    return ps[:, 3 * b + i // 2, (i % 2) * H:(i % 2 + 1) * H]
                v.tensor_scalar(mod[:, b, M_CA], blk(CA), 1.0, None, ALU.add)
                v.tensor_copy(mod[:, b, M_SA], blk(SA))
                for m, i in ((M_GA, GA), (M_GB, GB)):
                    v.tensor_scalar(gtmp[:, 0], blk(i), 0.0, 2.0, ALU.is_ge, ALU.mult)
                    step(v.tensor_scalar(gtmp[:, 1], blk(i), -1.0, FLOOR, ALU.mult, ALU.max))
                    step(v.tensor_tensor(gtmp[:, 1], blk(i), gtmp[:, 1], ALU.max))
                    step(v.scalar_tensor_tensor(mod[:, b, m], gtmp[:, 0], -1.0, gtmp[:, 1], ALU.add, ALU.mult))
                step(v.tensor_tensor(gabo[:, b], mod[:, b, M_GA], rs[:, R_BO:R_BO + H], ALU.mult))
            cview = ps[:, 6, 0:2 * KC * B].rearrange("p (m k b) -> p m k b", m=2, k=KC)
            v.tensor_copy(modc[:, 0], cview[:, 0])
            v.tensor_scalar(modc[:, 1], cview[:, 1], 1.0, None, ALU.add).then_inc(mod_done, 1)
            dve.wait_ge(mod_done, 1)

            dve.wait_ge(x_in, 16 * B * CHUNKS)
            LN = 7

            def normalise(src, b, at, nth):
                for t in range(TILES):
                    last = v.bn_stats(stats[b][:, t, :], src(t))
                last.then_inc(dve_step, 1)
                wait_apart(dve, dve_step, at + 1)
                for t in range(TILES):
                    last = v.bn_aggr(mv[b][:, t, :], stats[b][:, t, :])
                last.then_inc(dve_step, 1)
                dve.wait_ge(dve_step, at + 2)
                v.tensor_scalar(var[b], mv[b][:, :, 1], EPS, None, ALU.add).then_inc(var_ready, 1)
                dve.wait_ge(std_ready, nth + 1)
                v.reciprocal(rstd[b], std[b]).then_inc(dve_step, 1)
                dve.wait_ge(dve_step, at + 3)
                v.tensor_tensor(std[b], rstd[b], rstd[b], ALU.mult).then_inc(dve_step, 1)
                dve.wait_ge(dve_step, at + 4)
                v.tensor_tensor(std[b], std[b], var[b], ALU.mult).then_inc(dve_step, 1)
                dve.wait_ge(dve_step, at + 5)
                v.tensor_scalar(std[b], std[b], -0.5, 1.5, ALU.mult, ALU.add).then_inc(dve_step, 1)
                dve.wait_ge(dve_step, at + 6)
                v.tensor_tensor(rstd[b], rstd[b], std[b], ALU.mult).then_inc(dve_step, 1)
                dve.wait_ge(dve_step, at + 7)

            def centred(dst, src, b, t):
                return v.tensor_scalar(dst, src, mv[b][:, t, 0:1], rstd[b][:, t:t + 1], ALU.subtract, ALU.mult)

            base = count[0]
            per = B * (2 * LN + 4 * 2)
            with dve.Fori(0, CHUNKS) as c:
                at0 = c * per + base
                for b in range(B):
                    normalise(lambda t: xs[:, b, ds(c * TILES + t, 1), :].rearrange("p t f -> p (t f)"),
                              b, at0 + b * LN, c * (2 * B) + b)
                    for t in range(TILES):
                        last = centred(h_tile[:, b, t, :],
                                       xs[:, b, ds(c * TILES + t, 1), :].rearrange("p t f -> p (t f)"), b, t)
                    last.then_inc(ln1_done, 1)
                for b in range(B):
                    dve.wait_ge(h_ready, c * B + (b + 1))
                    normalise(lambda t: h_tile[:, b, t, :], b, at0 + (B * LN + b * LN),
                              c * (2 * B) + (B + b))
                    for t in range(TILES):
                        last = centred(y_tile[:, b, t, :], h_tile[:, b, t, :], b, t)
                    last.then_inc(y_ready, 1)
                for b in range(B):
                    for o in range(4):
                        at = at0 + (2 * B * LN + (4 * b + o) * 2)
                        dve.wait_ge(part1_ready, c * (4 * B) + (4 * b + o + 1))
                        v.tensor_tensor(rest[:, o % 2, :], qk_f[:, o, :], parts[:, b, o, 0, :],
                                        ALU.subtract).then_inc(dve_step, 1)
                        dve.wait_ge(dve_step, at + 1)
                        v.tensor_copy(parts[:, b, o, 1, :], rest[:, o % 2, :]).then_inc(dve_step, 1)
                        dve.wait_ge(dve_step, at + 2)
                        v.tensor_tensor(parts[:, b, o, 2, :], rest[:, o % 2, :], parts[:, b, o, 1, :],
                                        ALU.subtract).then_inc(parts_ready, 1)
                    for u in range(2):
                        dve.wait_ge(v_mm, c * (2 * B) + (2 * b + u + 1))
                        last = v.tensor_tensor(
                            v_heads[:, b * HEADS:(b + 1) * HEADS, ds(c * TILES + 2 * u, 2), :].rearrange(
                                "p h t d -> p t h d"),
                            ps[:, 6 + u, :].rearrange("p (t h d) -> p t h d", t=2, d=HD),
                            on_two(rs[:, R_BV:R_BV + H], 2).rearrange("p t (h d) -> p t h d", d=HD), ALU.add)
                        last.then_inc(v_ready, 1)
                for b in range(B):
                    dve.wait_ge(parts_out[b], (c + 1) * (16 * 4))
                dve.wait_ge(xr_done, c * B + B)
            base += per * CHUNKS

            def maximum(n, par, o):
                dve.wait_ge(scores_mm, n * OPS + (o + 1))
                if o == 0 and not (isinstance(n, int) and n < 2):
                    dve.wait_ge(top_done, n - 1)
                v.tensor_reduce(mx[par][:, o // 2, o % 2:o % 2 + 1], ps[:, 2 * (o % 2):2 * (o % 2) + 2, :],
                                AX.XY, ALU.max).then_inc(max_done, 1)

            def top(n, par, fresh):
                dve.wait_ge(max_done, (n + 1) * OPS)
                if not fresh:
                    dve.wait_ge(m_parts, n - 1)
                v.tensor_reduce(mtop[par], mx[par], AX.X, ALU.max).then_inc(top_done, 1)

            def context(n, at, par):
                dve.wait_ge(ctx_mm, n + 1)
                v.reciprocal(rec[par], ctx_ps[:, :, HD]).then_inc(dve_step, 1)
                dve.wait_ge(dve_step, at + 1)
                v.tensor_tensor(ctx_q[:, ds(n * TILES, TILES), :], ctx_ps[:, :, 0:HD],
                                rec[par].unsqueeze(2).to_broadcast([P, TILES, HD]),
                                ALU.mult).then_inc(ctx_done, 1)

            def steps(i, first, last):
                for s in range(2):
                    for c in range(CHUNKS):
                        n = i * (2 * CHUNKS) + (s * CHUNKS + c)
                        for o in range(OPS):
                            if not (last and s == 1 and c >= 2):
                                maximum(n + 2, c % 2, o)
                            if o == 0 and not (last and s == 1 and c == CHUNKS - 1):
                                top(n + 1, (c + 1) % 2, first and s == 0 and c == 0)
                            if o == 1 and not (first and s == 0 and c < 2):
                                context(n - 2, n + (base - 2), c % 2)
                            if o == 4 and not (last and s == 1 and c == CHUNKS - 1):
                                dve.wait_ge(mt_mm, n + 2)
                                par = (c + 1) % 2
                                if not (first and s == 0 and c == 0):
                                    dve.wait_ge(m_in[par], (i * CHUNKS + (s * CHUNKS + c + 1 - par) // 2)
                                                * (PARTS * 16))
                                v.tensor_copy(mrows[par][:, :], mt_ps).then_inc(mt_copied, 1)

            for n in range(2):
                for o in range(OPS):
                    maximum(n, n, o)
                if n == 0:
                    top(0, 0, True)
            dve.wait_ge(mt_mm, 1)
            v.tensor_copy(mrows[0][:, :], mt_ps).then_inc(mt_copied, 1)
            steps(0, True, False)
            with dve.Fori(1, HEADROWS // 2 - 1) as i:
                steps(i, False, False)
            steps(HEADROWS // 2 - 1, False, True)
            for n in (STEPS - 2, STEPS - 1):
                context(n, n + base, n % 2)
            base += STEPS

            per = B * (1 + LN + 13)
            with dve.Fori(0, CHUNKS) as c:
                at0 = c * per + base
                k0 = [0]

                def link(ins, apart=False):
                    ins.then_inc(dve_step, 1)
                    k0[0] += 1
                    if apart:
                        wait_apart(dve, dve_step, at0 + k0[0])
                    else:
                        dve.wait_ge(dve_step, at0 + k0[0])

                for b in range(B):
                    dve.wait_ge(proj_mm, c * B + (b + 1))
                    for u in range(2):
                        last = v.tensor_tensor(z_tile[b][:, 2 * u:2 * u + 2, :],
                                               ps[:, 2 + u, :].rearrange("p (t f) -> p t f", f=H),
                                               on_two(mod[:, b, M_GA], 2), ALU.mult)
                    last.then_inc(proj_read, 1)
                    dve.wait_ge(proj_read, c * B + (b + 1))
                    xt = xs[:, b, ds(c * TILES, TILES), :]
                    link(v.tensor_tensor(xt, xt, z_tile[b], ALU.add), True)
                    normalise(lambda t: xs[:, b, ds(c * TILES + t, 1), :].rearrange("p t f -> p (t f)"),
                              b, at0 + k0[0], c * B + (2 * B * CHUNKS + b))
                    k0[0] += LN
                    for t in range(TILES):
                        last = centred(z_tile[b][:, t, :],
                                       xs[:, b, ds(c * TILES + t, 1), :].rearrange("p t f -> p (t f)"), b, t)
                    last.then_inc(z_ready, 1)
                for b in range(B):
                    dve.wait_ge(gate_mm, c * B + (b + 1))
                    link(v.tensor_tensor(gl[b], ps[:, 6, 0:TILES * EXPERTS].rearrange("p (t e) -> p t e", e=EXPERTS),
                                         on_two(rs[:, R_GB:R_GB + EXPERTS], TILES), ALU.add))
                    link(v.tensor_reduce(g1[b], gl[b], AX.X, ALU.max))
                    v.tensor_tensor(gl[b], gl[b], g1[b].unsqueeze(2).to_broadcast([P, TILES, EXPERTS]),
                                    ALU.subtract).then_inc(gl_ready, 1)
                for b in range(B):
                    dve.wait_ge(ge_ready, c * B + (b + 1))
                    wide = [P, TILES, EXPERTS]
                    iota = on_two(cs[:, C_IOTA:C_IOTA + EXPERTS], TILES)
                    link(v.tensor_reduce(g1[b], gp[b], AX.X, ALU.add))
                    link(v.reciprocal(rec[b], g1[b]))
                    link(v.tensor_tensor(gp[b], gp[b], rec[b].unsqueeze(2).to_broadcast(wide), ALU.mult), True)
                    for t in range(TILES):
                        last = v.max(gtop[b][:, t, :], gp[b][:, t, :])
                    link(last, True)
                    for t in range(TILES):
                        last = v.max_index(gidx[b][:, t, :], gtop[b][:, t, :], gp[b][:, t, :])
                    link(last)
                    link(v.tensor_copy(gidf[b][:, :, :], gidx[b][:, :, :]))
                    link(v.tensor_tensor(gcw[b], iota, gidf[b][:, :, 0:1].to_broadcast(wide), ALU.is_equal))
                    link(v.tensor_tensor(gcw[b], gcw[b], gp[b][:, :, 0:1].to_broadcast(wide), ALU.mult))
                    link(v.tensor_tensor(gtop[b], iota, gidf[b][:, :, 1:2].to_broadcast(wide), ALU.is_equal))
                    link(v.tensor_tensor(gtop[b], gtop[b], gp[b][:, :, 1:2].to_broadcast(wide), ALU.mult))
                    link(v.tensor_tensor(gcw[b], gcw[b], gtop[b], ALU.add))
                    v.tensor_copy(cw[:, b, ds(c * TILES, TILES), :], gcw[b]).then_inc(cw_ready, 1)
                    dve.wait_ge(cwt_mm, c * B + (b + 1))
                    v.tensor_copy(cwt[b][:, :], ps[0:EXPERTS, 7, :]).then_inc(cwt_ready, 1)
                assert k0[0] == per, (k0[0], per)
            base += per * CHUNKS

            dve.wait_ge(acc_init, B * CHUNKS)
            v.memset(free_at_first[:, 0:1], 0.0).then_inc(l2_out, 4)
            v.memset(free_at_first[:, 1:2], 0.0).then_inc(l3_out, 4)
            with dve.Fori(0, EXPERTS // 2) as e2:
                for s in range(2):
                    with dve.Fori(0, CHUNKS) as c:
                        f4 = e2 * (8 * CHUNKS) + c * 4 + s * (4 * CHUNKS)
                        for b in range(B):
                            for fo in range(KC):
                                dve.wait_ge(l2_mm, f4 + (2 * b + fo + 1))
                                v.tensor_scalar(hid[:, 1, b, fo, :], ps[:, 2 * b + fo, :],
                                                cs[:, ds(e2 * (2 * KC) + (C_B2 + s * KC + fo), 1)], 0.0,
                                                ALU.add, ALU.max).then_inc(l2_out, 1)
                        for b in range(B):
                            for u in range(2):
                                dve.wait_ge(l3_mm, f4 + (2 * b + u + 1))
                                for t in (2 * u, 2 * u + 1):
                                    tile = acc[:, b, ds(c * TILES + t, 1), :].rearrange("p t f -> p (t f)")
                                    w = cw[:, b, ds(c * TILES + t, 1), ds(e2 * 2 + s, 1)].rearrange(
                                        "p t e -> p (t e)")
                                    last = v.scalar_tensor_tensor(
                                        tile, ps[:, 4 + 2 * b + u, (t % 2) * H:(t % 2 + 1) * H], w, tile,
                                        ALU.mult, ALU.add)
                                last.then_inc(l3_out, 1)

            dve.wait_ge(l3_out, 4 * FLAT + 4)
            with dve.Fori(0, CHUNKS) as c:
                for b in range(B):
                    a = acc[:, b, ds(c * TILES, TILES), :]
                    v.tensor_tensor(a, a, on_two(mod[:, b, M_GB], TILES), ALU.mult).then_inc(dve_step, 1)
                    dve.wait_ge(dve_step, c * B + (base + b + 1))
                    v.tensor_tensor(o_tile[:, b], a, xs[:, b, ds(c * TILES, TILES), :],
                                    ALU.add).then_inc(o_ready, 1)
                for b in range(B):
                    dve.wait_ge(o_out[b], (c + 1) * 16)

        @block.gpsimd
        def _(pool):
            g = nc.gpsimd
            pool.wait_ge(mod_done, 1)
            with pool.Fori(0, CHUNKS) as c:
                per = 3 * B
                for b in range(B):
                    h = h_tile[:, b]
                    pool.wait_ge(ln1_done, c * B + (b + 1))
                    g.tensor_tensor(h, h, on_two(mod[:, b, M_CA], TILES), ALU.mult).then_inc(pool_step, 1)
                    pool.wait_ge(pool_step, c * per + (b + 1))
                    g.tensor_tensor(h, h, on_two(mod[:, b, M_SA], TILES), ALU.add).then_inc(h_ready, 1)
                for b in range(B):
                    pool.wait_ge(h_ready, c * B + (b + 1))
                    at = c * per + (B + 2 * b)
                    r = xr_tile[:, b]
                    xt = xs[:, b, ds(c * TILES, TILES), :]
                    g.tensor_tensor(r, h_tile[:, b], on_two(mod[:, b, M_GA], TILES), ALU.mult).then_inc(pool_step, 1)
                    pool.wait_ge(pool_step, at + 1)
                    g.tensor_tensor(r, r, on_two(gabo[:, b], TILES), ALU.add).then_inc(pool_step, 1)
                    pool.wait_ge(pool_step, at + 2)
                    g.tensor_tensor(xt, xt, r, ALU.add).then_inc(xr_done, 1)
            base = 3 * B * CHUNKS

            def stage_v(gi, s):
                g.tensor_copy(vs[:, s, :, 0:HD], v_heads[:, ds(gi, 1), :, :].rearrange(
                    "p g t d -> p (g t) d")).then_inc(v_staged, 1)

            STEP = 5

            def m_prepare(n, par, fresh):
                at = n * STEP + base
                if not fresh:
                    pool.wait_ge(mt_mm, n - 1)
                wait_apart(pool, top_done, n + 1)
                pa = mparts[par]
                g.tensor_scalar(mneg, mtop[par], -1.0, None, ALU.mult).then_inc(pool_step, 1)
                wait_apart(pool, pool_step, at + 1)
                g.tensor_copy(pa[:, 0, :], mneg).then_inc(pool_step, 1)
                pool.wait_ge(pool_step, at + 2)
                g.tensor_tensor(mres, mneg, pa[:, 0, :], ALU.subtract).then_inc(pool_step, 1)
                wait_apart(pool, pool_step, at + 3)
                g.tensor_copy(pa[:, 1, :], mres).then_inc(pool_step, 1)
                pool.wait_ge(pool_step, at + 4)
                g.tensor_tensor(mres2, mres, pa[:, 1, :], ALU.subtract).then_inc(pool_step, 1)
                wait_apart(pool, pool_step, at + 5)
                g.tensor_copy(pa[:, 2, :], mres2).then_inc(m_parts, 1)

            def steps(i, first, last):
                for s in range(2):
                    for c in range(CHUNKS):
                        n = i * (2 * CHUNKS) + (s * CHUNKS + c)
                        if c == 1 and not (last and s == 1):
                            if not (first and s == 0):
                                wait_apart(pool, pv_mm, (i * 2 + s) * (CHUNKS * QUADS))
                            stage_v(i * 2 + (s + 1), 1 - s)
                        if not (last and s == 1 and c == CHUNKS - 1):
                            m_prepare(n + 1, (c + 1) % 2, first and s == 0 and c == 0)

            pool.wait_ge(v_ready, 2 * B * CHUNKS)
            pool.wait_ge(fixed_done, 1)
            stage_v(0, 0)
            m_prepare(0, 0, True)
            steps(0, True, False)
            with pool.Fori(1, HEADROWS // 2 - 1) as i:
                steps(i, False, False)
            steps(HEADROWS // 2 - 1, False, True)


def kernel(**inputs):
    import ml_dtypes
    import numpy as np
    from concourse import bacc
    from concourse.bass_utils import run_bass_kernel_spmd

    a = {n.replace("L0_", ""): np.asarray(v) for n, v in inputs.items()}

    def columns(v):
        return v.reshape(-1, KC, P).transpose(2, 0, 1).reshape(P, -1)

    def repeated(v):
        return np.broadcast_to(v.reshape(1, -1), (P, v.size))

    cond = a["c"].reshape(B, KC, P).transpose(2, 1, 0).reshape(P, KC * B)
    sel = (np.arange(P)[:, None] % VW == np.arange(HD + 1)[None, :]).astype(np.float32)
    cols = np.concatenate([cond, columns(a["attn_b_qkv"][:2 * H]), columns(a["attn_ln_gamma"]),
                           columns(a["attn_ln_beta"]), columns(a["ffn_b1"]), columns(a["ffn_b2"]),
                           repeated(np.arange(EXPERTS, dtype=np.float32)), sel], axis=1)
    rows = np.concatenate([repeated(a["attn_b_qkv"][2 * H:]), repeated(a["attn_b_out"]),
                           repeated(a["ffn_gate_b"])], axis=1)
    eye = np.eye(P, dtype=np.float32)
    arrays = {
        "x": a["attn_hidden_states"], "cols": cols, "rows": rows, "wmod": a["wmod"],
        "wqkv_t": a["attn_W_qkv"].T, "wout_t": a["attn_W_out"].T, "gate_t": a["ffn_gate_w"].T,
        "w1": a["ffn_w1"], "w2": a["ffn_w2"], "w3": a["ffn_w3"], "b3": a["ffn_b3"],
        "ident": eye, "ident_b": eye.astype(ml_dtypes.bfloat16),
    }
    arrays = {n: np.ascontiguousarray(v) for n, v in arrays.items()}
    nc = bacc.Bacc("TRN2", target_bir_lowering=False, num_devices=1)
    aps = {n: nc.dram_tensor(n, v.shape, mybir.dt.from_np(v.dtype), kind="ExternalInput").ap()
           for n, v in arrays.items()}
    out = nc.dram_tensor("out", (B, S, H), mybir.dt.float32, kind="ExternalOutput").ap()
    build(nc, out=out, **aps)
    return run_bass_kernel_spmd(nc, [arrays], core_ids=[0]).results[0]["out"]
```

```python
import concourse.bass as bass
from concourse import mybir
from contextlib import ExitStack

P = 128
B, S, H = 2, 2048, 256
HEADS, HD = 16, 16
EXPERTS = 8
EPS = 1e-5
FLOOR = 0.25
KC = H // P
CHUNK = 512
CHUNKS = S // CHUNK
TILES = CHUNK // P
STILES = S // P
HEADROWS = B * HEADS
PARTS = 3
TERMS = 6
TROWS = TERMS * HD
HEAD_DMAS = 2 * TERMS
VW = 32
C_COND, C_BQK, C_LNG, C_LNB = 0, 4, 8, 10
C_EB = 12
C_IOTA = 44
NCOLS = 52
R_BV, R_BO, R_GB = 0, H, 2 * H
NROWS = 2 * H + EXPERTS
SA, CA, GA, SB_, CB, GB = range(6)
M_CA, M_SA, M_GA, M_GB = range(4)


def build(nc, x, cols, rows, wmod, wqkv_t, wout_t, gate_t, w1, w2, w3, b3, ident, ident_b, out):
    f32, f32r, bf16, u32 = mybir.dt.float32, mybir.dt.float32r, mybir.dt.bfloat16, mybir.dt.uint32
    ALU, ACT, AX = mybir.AluOpType, mybir.ActivationFunctionType, mybir.AxisListType
    ds = bass.ds
    ctx = ExitStack()

    def sb(name, shape, dt=f32):
        return ctx.enter_context(nc.sbuf_tensor(name, shape, dt))

    def sem(name):
        return ctx.enter_context(nc.semaphore(name))

    with ctx:
        q_parts = nc.dram_tensor("q_parts", [PARTS, HEADROWS * HD, S], bf16, kind="Internal").ap()
        k_parts = nc.dram_tensor("k_parts", [PARTS, HEADROWS * HD, S], bf16, kind="Internal").ap()

        xs = sb("xs", [P, B, STILES, H])
        cs = sb("cs", [P, NCOLS])
        rs = sb("rs", [P, NROWS])
        mod = sb("mod", [P, B, 4, H])
        gah = sb("gah", [P, B, 2, H])
        mean1 = sb("mean1", [P, B, STILES])
        rstd1 = sb("rstd1", [P, B, STILES])
        modc = sb("modc", [P, 2, KC, B])
        wout = sb("wout", [P, KC, H])
        gatew = sb("gatew", [P, KC, EXPERTS])
        b3s = sb("b3s", [EXPERTS, H])
        idf = sb("idf", [P, P])
        idb = sb("idb", [P, P], bf16)
        cw = sb("cw", [P, B, STILES, EXPERTS])
        small = sb("small", [P, 384])
        raw = sb("raw", [P, 3, KC, H])
        exb = sb("exb", [P, 2, 2 * KC])
        t3 = sb("t3", [P, 4 * TILES * H])

        at = [0]

        def piece(n):
            at[0] += n
            return small[:, at[0] - n:at[0]]

        stats = [piece(TILES * 6).rearrange("p (t n) -> p t n", n=6) for _ in range(B)]
        mv = [piece(TILES * 2).rearrange("p (t n) -> p t n", n=2) for _ in range(B)]
        rstd = [piece(TILES) for _ in range(B)]
        var = [piece(TILES) for _ in range(B)]
        std = [piece(TILES) for _ in range(B)]
        mx = [piece(16).rearrange("p (t n) -> p t n", n=4) for _ in range(2)]
        silu = piece(4)
        mtop = [piece(4) for _ in range(2)]
        mneg = piece(4)
        mres = piece(4)
        mres2 = piece(4)
        sig = piece(4)
        free_at_first = piece(3)
        ctx_sum = [piece(TILES * (HD + 1)).rearrange("p (t n) -> p t n", t=TILES) for _ in range(2)]
        rec = [piece(4) for _ in range(B)]
        logits = sb("logits", [P, B, STILES, EXPERTS])
        mparts = [sb(f"mparts{n}", [P, PARTS, TILES], bf16) for n in range(2)]
        mrows = [sb(f"mrows{n}", [PARTS * TILES, P], bf16) for n in range(2)]
        b3g = sb("b3g", [EXPERTS, B, H])

        early = ExitStack()

        def sb_early(name, shape, dt=f32):
            return early.enter_context(nc.sbuf_tensor(name, shape, dt))

        vall = sb_early("vall", [P, HEADROWS * STILES * HD])
        pall = sb_early("pall", [P, STILES * CHUNK])
        q6 = sb_early("q6", [P, 2, S], bf16)
        k6 = sb_early("k6", [P, 2, S], bf16)
        vs = sb_early("vs", [P, 2, STILES, VW])
        acc_sb = sb_early("acc_sb", [P, 2, CHUNK])
        xr = sb_early("xr", [P, B, H])
        early.close()
        late = ExitStack()

        def sb_late(name, shape, dt=f32):
            return late.enter_context(nc.sbuf_tensor(name, shape, dt))

        ht_h = sb_late("ht_h", [P, KC, B, S], f32r)
        ht_l = sb_late("ht_l", [P, KC, B, S], f32r)
        wx_h = sb_late("wx_h", [P, 2, 4, KC, H], f32r)
        wx_l = sb_late("wx_l", [P, 2, 4, KC, H], f32r)
        with nc.sbuf_tensor("call", [P, HEADROWS * STILES * HD], f32) as call:
            pass
        hid_h = sb_late("hid_h", [P, 2, B, KC, CHUNK], f32r)
        hid_l = sb_late("hid_l", [P, 2, B, KC, CHUNK], f32r)
        late.close()

        v_heads = vall[:, :].rearrange("p (g t d) -> p g t d", t=STILES, d=HD)
        ctx_q = call[:, :].rearrange("p (n d) -> p n d", d=HD)
        ctx_h = call[:, :].rearrange("p (b h t d) -> p b h t d", b=B, h=HEADS, d=HD)
        s1 = call[:, :].rearrange("p (u b n) -> p u b n", u=4, b=B)
        h_tile = s1[:, 0].rearrange("p b (t f) -> p b t f", f=H)
        y_tile = s1[:, 1].rearrange("p b (t f) -> p b t f", f=H)
        xn_t = s1[:, 2].rearrange("p b (k s) -> p b k s", k=KC)
        wm = call[:, 4096:4096 + KC * 6 * H].rearrange("p (k n) -> p k n", k=KC)
        qk_f = pall[:, 0:4 * CHUNK].rearrange("p (o s) -> p o s", o=4)
        parts = pall[:, 4 * CHUNK:].bitcast(bf16).rearrange("p (b o r s) -> p b o r s", b=B, o=4, r=PARTS)
        rest = acc_sb
        prob = pall[:, :].rearrange("p (k s) -> p k s", s=CHUNK)
        t3v = t3[:, :].rearrange("p (u n) -> p u n", u=4)
        k6f = k6[:, :, :].bitcast(f32)
        wqkv = t3[:, 2 * TILES * H:2 * TILES * H + KC * 3 * H].rearrange("p (k n) -> p k n", k=KC)
        c_tile = [k6f[:, b].rearrange("p (t f) -> p t f", f=H) for b in range(B)]
        z_tile = [t3v[:, b].rearrange("p (t f) -> p t f", f=H) for b in range(B)]
        hc_t = ctx_t = [t3v[:, 2 + b].rearrange("p (k s) -> p k s", k=KC) for b in range(B)]
        cwt = [t3v[0:EXPERTS, 2 + n, 0:CHUNK] for n in range(2)]
        h_full = t3v[:, 0].rearrange("p (n s) -> p n s", n=2)
        cond_b = t3v[:, 0, 0:KC * B * P].rearrange("p (k b n) -> p k b n", k=KC, b=B)
        gtmp = t3v[:, 1, 0:2 * H].rearrange("p (a n) -> p a n", a=2)
        gate_t5 = [t3v[:, 0, n * 256:(n + 1) * 256].rearrange("p (t e) -> p t e", e=EXPERTS) for n in range(4)]
        gate_p = logits[:, :, :, :].rearrange("p b t e -> p (b t) e")
        gate_s = [t3v[:, 1, n * 32:(n + 1) * 32] for n in range(4)]
        w3g = t3v[:, 1, 0:KC * H].rearrange("p (k f) -> p k f", k=KC)

        ps = ctx.enter_context(nc.psum_tensor("ps", [P, 8, CHUNK], f32))
        MISC, ACC = 7, 6
        RING = [u % 3 for u in range(15)] + [1]
        BACK = [4, 2, 4] + [3] * 12 + [2]
        SCORE, ST = 0, 3
        acc_ps = ps[:, ACC, :]
        ctx_ps = ps[:, MISC, :].rearrange("p (t g n) -> p t g n", t=TILES, g=4)
        mt_ps = ps[0:PARTS * TILES, MISC, 0:P // 2].bitcast(bf16)

        cols_in = sem("cols_in")
        const_in = sem("const_in")
        x_in = [sem(f"x_in{n}") for n in range(2)]
        wmod_in = sem("wmod_in")
        sig_done = sem("sig_done")
        cond_done = sem("cond_done")
        mod_mm = sem("mod_mm")
        mod_done = sem("mod_done")
        fixed_done = sem("fixed_done")
        dve_step = sem("dve_step")
        pool_step = sem("pool_step")
        var_ready = sem("var_ready")
        std_ready = sem("std_ready")
        ln1_done = sem("ln1_done")
        h_ready = sem("h_ready")
        xr_step = sem("xr_step")
        xr_done = sem("xr_done")
        rest_ready = sem("rest_ready")
        y_ready = sem("y_ready")
        xt_mm = sem("xt_mm")
        xn_ready = sem("xn_ready")
        qk_mm = sem("qk_mm")
        v_mm = sem("v_mm")
        part1_ready = sem("part1_ready")
        parts_ready = sem("parts_ready")
        v_ready = sem("v_ready")
        parts_out = [sem(f"parts_out{b}") for b in range(B)]
        head_in = [sem(f"head_in{s}") for s in range(2)]
        v_staged = sem("v_staged")
        scores_mm = sem("scores_mm")
        max_done = sem("max_done")
        top_done = sem("top_done")
        m_parts = sem("m_parts")
        mt_mm = sem("mt_mm")
        mt_copied = sem("mt_copied")
        m_in = [sem(f"m_in{s}") for s in range(2)]
        st_mm = sem("st_mm")
        exp_done = sem("exp_done")
        pv_mm = sem("pv_mm")
        acc_out = sem("acc_out")
        ctx_mm = sem("ctx_mm")
        ctx_read = sem("ctx_read")
        rec_ready = sem("rec_ready")
        ctx_done = sem("ctx_done")
        c_copied = sem("c_copied")
        ct_mm = sem("ct_mm")
        ct_ready = sem("ct_ready")
        proj_mm = sem("proj_mm")
        proj_read = sem("proj_read")
        z_ready = sem("z_ready")
        ht_mm = sem("ht_mm")
        ht_ready = sem("ht_ready")
        gate_mm = sem("gate_mm")
        gl_read = sem("gl_read")
        logits_less = sem("logits_less")
        gate_exp = sem("gate_exp")
        cw_done = sem("cw_done")
        cwt_mm = sem("cwt_mm")
        cwt_ready = sem("cwt_ready")
        b3_mm = sem("b3_mm")
        acc_init = sem("acc_init")
        ht_low = sem("ht_low")
        raw_in = sem("raw_in")
        w_step = sem("w_step")
        w_split = sem("w_split")
        h_mm = sem("h_mm")
        relu_out = sem("relu_out")
        low_out = sem("low_out")
        l3_mm = sem("l3_mm")
        l3_out = sem("l3_out")
        o_out = [sem(f"o_out{b}") for b in range(B)]

        CONSTS = 7 * 16
        STEPS = HEADROWS * CHUNKS
        QUADS = STILES // 4
        OPS = 4 * TILES
        FLAT = EXPERTS * CHUNKS

        def wait_apart(eng, semaphore, value):
            eng.wait_ge(semaphore, value)
            eng.nop(nofuse=True)

        def on_two(ap, n):
            return ap.unsqueeze(1).to_broadcast([P, n, ap.shape[1]])

        block = ctx.enter_context(nc.Block())

        @block.sync
        def _(sp):
            sp.dma_start(cs[:, :], cols).then_inc(cols_in, 16)
            xv = x.rearrange("b (t p) f -> p b t f", p=P)
            for c in range(CHUNKS):
                for b in range(B):
                    t = ds(c * TILES, TILES)
                    sp.dma_start(xs[:, b, t, :], xv[:, b, t, :]).then_inc(x_in[c > 0], 16)
                if c == 0:
                    sp.dma_start(wm, wmod.rearrange("(k p) n -> p k n", p=P)).then_inc(wmod_in, 16)
                    sp.dma_start(rs[:, :], rows).then_inc(const_in, 16)
                    sp.dma_start(wqkv[:, :, :], wqkv_t.rearrange("(k p) n -> p k n", p=P)).then_inc(const_in, 16)
                    sp.dma_start(wout[:, :, :], wout_t.rearrange("(k p) n -> p k n", p=P)).then_inc(const_in, 16)
                    sp.dma_start(gatew[:, :, :], gate_t.rearrange("(k p) n -> p k n", p=P)).then_inc(const_in, 16)
                    sp.dma_start(b3s[:, :], b3).then_inc(const_in, 16)
                    sp.dma_start(idf[:, :], ident).then_inc(const_in, 16)
                    sp.dma_start(idb[:, :], ident_b).then_inc(const_in, 16)
            with sp.Fori(0, CHUNKS) as c:
                for b in range(B):
                    sp.wait_ge(parts_ready, c * (4 * B) + 4 * (b + 1))
                    for o in range(4):
                        row = (b * KC + o % KC) * P
                        dst = (q_parts, k_parts)[o // KC][:, row:row + P, ds(c * CHUNK, CHUNK)]
                        sp.dma_start(dst.rearrange("r p s -> p r s"), parts[:, b, o]).then_inc(parts_out[b], 16)

            def load_head(g, s):
                for term, (qr, kr) in enumerate(((0, 0), (0, 1), (0, 2), (1, 0), (1, 1), (2, 0))):
                    for dst, src, r in ((q6, q_parts, qr), (k6, k_parts, kr)):
                        sp.dma_start(dst[term * HD:(term + 1) * HD, s, :],
                                     src[r, ds(g * HD, HD), :]).then_inc(head_in[s], 16)

            def load_m(n, par, s, c):
                sp.wait_ge(mt_copied, n + 1)
                for r in range(PARTS):
                    sp.dma_start(q6[TROWS + r:TROWS + r + 1, s, c * CHUNK:(c + 1) * CHUNK],
                                 mrows[par][r * TILES:(r + 1) * TILES, :]).then_inc(m_in[par], 16)

            for b in range(B):
                sp.wait_ge(parts_out[b], 16 * 4 * CHUNKS)
            load_head(0, 0)
            load_m(0, 0, 0, 0)

            def steps(i, first, last):
                for s in range(2):
                    if not (last and s == 1):
                        if not (first and s == 0):
                            sp.wait_ge(st_mm, (i * 2 + s) * (CHUNKS * STILES))
                        load_head(i * 2 + (s + 1), 1 - s)
                    for c in range(CHUNKS):
                        if last and s == 1 and c == CHUNKS - 1:
                            continue
                        n = i * (2 * CHUNKS) + (s * CHUNKS + c)
                        load_m(n + 1, (c + 1) % 2, (s + (c + 1) // CHUNKS) % 2, (c + 1) % CHUNKS)

            steps(0, True, False)
            with sp.Fori(1, HEADROWS // 2 - 1) as i:
                steps(i, False, False)
            steps(HEADROWS // 2 - 1, False, True)

            def load_weights(e):
                for l, w in enumerate((w1, w2, w3)):
                    sp.dma_start(raw[:, l], w[e].rearrange("(k p) n -> p k n", p=P)).then_inc(raw_in, 16)

            load_weights(0)
            with sp.Fori(1, EXPERTS) as e:
                wait_apart(sp, w_split, e * 1)
                load_weights(e)
            ov = out.rearrange("b (t p) f -> p b t f", p=P)
            for c in range(CHUNKS):
                for b in range(B):
                    sp.wait_ge(l3_out, 4 * (FLAT - CHUNKS + c + 1) + 2 * (b + 1))
                    t = ds(c * TILES, TILES)
                    sp.dma_start(ov[:, b, t, :], xs[:, b, t, :]).then_inc(o_out[b], 16)
            for b in range(B):
                sp.wait_ge(o_out[b], 16 * CHUNKS)

        @block.tensor
        def _(pe):
            mm = nc.tensor.matmul
            pe.wait_ge(cond_done, 2)
            pe.wait_ge(wmod_in, 16)
            for b in range(B):
                for n in range(3):
                    for k in range(KC):
                        last = mm(ps[:, 3 * b + n, :], cond_b[:, k, b, :], wm[:, k, n * CHUNK:(n + 1) * CHUNK],
                                  start=(k == 0), stop=(k == KC - 1))
            for kind, blk in enumerate((SB_, CB)):
                for f in range(KC):
                    for k in range(KC):
                        col = (kind * KC + f) * B
                        last = mm(ps[:, 6, col:col + B], wm[:, k, blk * H + f * P:blk * H + (f + 1) * P],
                                  cond_b[:, k, :, 0], start=(k == 0), stop=(k == KC - 1))
            last.then_inc(mod_mm, 1)

            pe.wait_ge(const_in, CONSTS)
            pe.wait_ge(mod_done, 1)

            def project(c, first):
                for b in range(B):
                    pe.wait_ge(y_ready, c * B + (b + 1))
                    if not (first and b == 0):
                        pe.wait_ge(xn_ready, c * (2 * B) + 2 * b)
                    for k in range(KC):
                        for t in range(TILES):
                            last = nc.tensor.transpose(ps[:, k, t * P:(t + 1) * P],
                                                       y_tile[:, b, t, k * P:(k + 1) * P], idf[:, :])
                    last.then_inc(xt_mm, 1)
                for b in range(B):
                    pe.wait_ge(xn_ready, c * (2 * B) + 2 * (b + 1))
                    for o in range(4):
                        if not (first and b == 0):
                            pe.wait_ge(part1_ready, c * (4 * B) + (4 * b + o - 3))
                        for k in range(KC):
                            last = mm(ps[:, 2 + o, :], wqkv[:, k, o * P:(o + 1) * P], xn_t[:, b, k, :],
                                      start=(k == 0), stop=(k == KC - 1))
                        last.then_inc(qk_mm, 1)
                    for u in range(2):
                        if not (first and b == 0):
                            pe.wait_ge(v_ready, c * (2 * B) + (2 * b + u - 1))
                        for t in (2 * u, 2 * u + 1):
                            for k in range(KC):
                                last = mm(ps[:, 6 + u, (t % 2) * H:(t % 2 + 1) * H],
                                          xn_t[:, b, k, t * P:(t + 1) * P], wqkv[:, k, 2 * H:3 * H],
                                          start=(k == 0), stop=(k == KC - 1))
                        last.then_inc(v_mm, 1)

            project(0, True)
            with pe.Fori(1, CHUNKS) as c:
                project(c, False)

            def scores(n, s, c, u):
                t, kb = u // 4, u % 4
                if not (isinstance(n, int) and n == 0 and u < 3):
                    pe.wait_ge(max_done, n * OPS + (u - BACK[u] + 1))
                q0 = c * CHUNK + t * P
                mm(ps[:, SCORE + RING[u], :], q6[0:TROWS, s, q0:q0 + P],
                   k6[0:TROWS, s, kb * CHUNK:(kb + 1) * CHUNK], start=True, stop=True).then_inc(scores_mm, 1)

            def m_transpose(n, par):
                pe.wait_ge(m_parts, n + 1)
                nc.tensor.transpose(mt_ps, mparts[par][:, :, :].rearrange("p r t -> p (r t)"),
                                    idb[:, :]).then_inc(mt_mm, 1)

            def pv(n, s, q):
                pe.wait_ge(exp_done, n * STILES + 4 * (q + 1))
                if q == 0 and not (isinstance(n, int) and n == 0):
                    pe.wait_ge(acc_out, n)
                for j in range(4):
                    k = 4 * q + j
                    last = mm(ps[32 * j:32 * (j + 1), ACC, :], vs[:, s, k, :], prob[:, k, :],
                              start=(q == 0), stop=(q == QUADS - 1))
                last.then_inc(pv_mm, 1)

            def ctx_out(n, par):
                pe.wait_ge(acc_out, n + 1)
                for t in range(TILES):
                    last = nc.tensor.transpose(ps[:, MISC, t * P:(t + 1) * P], acc_sb[:, par, t * P:(t + 1) * P],
                                               idf[:, :])
                last.then_inc(ctx_mm, 1)

            def steps(i, first, last):
                for s in range(2):
                    for c in range(CHUNKS):
                        n = i * (2 * CHUNKS) + (s * CHUNKS + c)
                        step0 = first and s == 0 and c == 0
                        c2, s2 = (c + 2) % CHUNKS, (s + (c + 2) // CHUNKS) % 2
                        ahead = not (last and s == 1 and c >= 2)
                        if c == 0:
                            pe.wait_ge(v_staged, i * 2 + (s + 1))
                        if c == 2 and ahead:
                            pe.wait_ge(head_in[s2], (i + (s + 1) // 2 + 1) * (HEAD_DMAS * 16))
                        pe.wait_ge(m_in[c % 2], (i * CHUNKS + (s * CHUNKS + c) // 2 + 1) * (PARTS * 16))
                        for q in range(QUADS):
                            for j in range(4):
                                k = 4 * q + j
                                if not (step0 and k < 3):
                                    pe.wait_ge(exp_done, n * STILES + (k - BACK[k] + 1))
                                mm(ps[:, ST + RING[k], :], k6[0:TROWS + PARTS, s, k * P:(k + 1) * P],
                                   q6[0:TROWS + PARTS, s, c * CHUNK:(c + 1) * CHUNK],
                                   start=True, stop=True).then_inc(st_mm, 1)
                                if ahead:
                                    scores(n + 2, s2, c2, k)
                            if q == 0:
                                if not step0:
                                    pv(n - 1, (s + (c - 1) // CHUNKS) % 2, QUADS - 1)
                            else:
                                pv(n, s, q - 1)
                            if q == 1 and not (last and s == 1 and c == CHUNKS - 1):
                                if not (first and s == 0 and c < 2):
                                    pe.wait_ge(ctx_read, n - 1)
                                m_transpose(n + 1, (c + 1) % 2)
                            if q == QUADS - 1 and not step0:
                                if not (last and s == 1 and c == CHUNKS - 1):
                                    pe.wait_ge(mt_copied, n + 2)
                                else:
                                    pe.wait_ge(ctx_read, n - 1)
                                ctx_out(n - 1, (c + 1) % 2)

            pe.wait_ge(fixed_done, 1)
            pe.wait_ge(head_in[0], HEAD_DMAS * 16)
            pe.wait_ge(v_ready, 2 * B * CHUNKS)
            pe.wait_ge(part1_ready, 4 * B * CHUNKS)
            for n in range(2):
                for u in range(STILES):
                    scores(n, 0, n, u)
            m_transpose(0, 0)
            pe.wait_ge(mt_copied, 1)
            steps(0, True, False)
            with pe.Fori(1, HEADROWS // 2 - 1) as i:
                steps(i, False, False)
            steps(HEADROWS // 2 - 1, False, True)
            pv(STEPS - 1, 1, QUADS - 1)
            pe.wait_ge(ctx_read, STEPS - 1)
            ctx_out(STEPS - 1, 1)

            def front(c, first):
                for b in range(B):
                    pe.wait_ge(c_copied, c * B + (b + 1))
                    if b:
                        pe.wait_ge(ct_ready, c * (2 * B) + 2 * b)
                    elif not (isinstance(c, int) and c < 2):
                        pe.wait_ge(gl_read, (c - 1) * B)
                    for k in range(KC):
                        for t in range(TILES):
                            last = nc.tensor.transpose(ps[:, k, t * P:(t + 1) * P],
                                                       c_tile[b][:, t, k * P:(k + 1) * P], idf[:, :])
                    last.then_inc(ct_mm, 1)
                for b in range(B):
                    pe.wait_ge(ct_ready, c * (2 * B) + 2 * (b + 1))
                    if not first:
                        pe.wait_ge(proj_read, c * B + (b - 1))
                    for t in range(TILES):
                        for k in range(KC):
                            last = mm(ps[:, 2 + 2 * b + t // 2, (t % 2) * H:(t % 2 + 1) * H],
                                      ctx_t[b][:, k, t * P:(t + 1) * P], wout[:, k, :],
                                      start=(k == 0), stop=(k == KC - 1))
                    last.then_inc(proj_mm, 1)

            def back(c, first):
                for b in range(B):
                    pe.wait_ge(z_ready, c * B + (b + 1))
                    if not (first and b == 0):
                        pe.wait_ge(ht_ready, c * (2 * B) + 2 * b)
                    for k in range(KC):
                        for t in range(TILES):
                            last = nc.tensor.transpose(ps[:, 6 + k, t * P:(t + 1) * P],
                                                       z_tile[b][:, t, k * P:(k + 1) * P], idf[:, :])
                    last.then_inc(ht_mm, 1)
                for b in range(B):
                    pe.wait_ge(ht_ready, c * (2 * B) + 2 * (b + 1))
                    for t in range(TILES):
                        for k in range(KC):
                            last = mm(ps[:, b, t * EXPERTS:(t + 1) * EXPERTS],
                                      hc_t[b][:, k, t * P:(t + 1) * P], gatew[:, k, :],
                                      start=(k == 0), stop=(k == KC - 1))
                    last.then_inc(gate_mm, 1)

            front(0, True)
            front(1, False)
            back(0, True)
            with pe.Fori(1, CHUNKS - 1) as c:
                front(c + 1, False)
                back(c, False)
            back(CHUNKS - 1, False)
            for m in range(B * CHUNKS):
                b, c = m // CHUNKS, m % CHUNKS
                pe.wait_ge(cw_done, 1)
                if m >= 2:
                    pe.wait_ge(cwt_ready, m - 1)
                for t in range(TILES):
                    last = nc.tensor.transpose(ps[0:EXPERTS, 6 + m % 2, t * P:(t + 1) * P],
                                               cw[:, b, c * TILES + t, :], idf[:, :])
                last.then_inc(cwt_mm, 1)
                pe.wait_ge(cwt_ready, m + 1)
                if m >= 2:
                    pe.wait_ge(acc_init, m - 1)
                for t in range(TILES):
                    last = mm(ps[:, 2 + 2 * (m % 2) + t // 2, (t % 2) * H:(t % 2 + 1) * H],
                              cwt[m % 2][:, t * P:(t + 1) * P], b3g[:, b, :], start=True, stop=True)
                last.then_inc(b3_mm, 1)

            def three(o, stationary, moving):
                n = 0
                for k in range(KC):
                    for a, m in ((0, 0), (1, 0), (0, 1)):
                        last = mm(o, stationary[a](k), moving[m](k), start=(n == 0), stop=(n == 3 * KC - 1))
                        n += 1
                return last

            pe.wait_ge(ht_low, B * KC * CHUNKS)
            with pe.Fori(0, EXPERTS // 2) as e2:
                for s in range(2):
                    wait_apart(pe, w_split, e2 * 2 + (s + 1))
                    with pe.Fori(0, CHUNKS) as c:
                        f = e2 * (2 * CHUNKS) + c + s * CHUNKS
                        for b in range(B):
                            for fo in range(KC):
                                pe.wait_ge(relu_out, f * 8 + (2 * b + fo + 1))
                                three(ps[:, 2 * b + fo, :],
                                      [lambda k, w=w: w[:, s, 0, k, fo * P:(fo + 1) * P] for w in (wx_h, wx_l)],
                                      [lambda k, h=h: h[:, k, b, ds(c * CHUNK, CHUNK)] for h in (ht_h, ht_l)]
                                      ).then_inc(h_mm, 1)
                        for b in range(B):
                            pe.wait_ge(low_out, f * 8 + (2 * b + 4))
                            for fo in range(KC):
                                three(ps[:, 2 * b + fo, :],
                                      [lambda k, w=w: w[:, s, 1, k, fo * P:(fo + 1) * P] for w in (wx_h, wx_l)],
                                      [lambda k, h=h: h[:, 0, b, k, :] for h in (hid_h, hid_l)]).then_inc(h_mm, 1)
                        for b in range(B):
                            pe.wait_ge(low_out, f * 8 + (4 + 2 * b + 4))
                            for u in range(2):
                                pe.wait_ge(l3_out, f * 4 + (2 * b + u + 1))
                                for t in (2 * u, 2 * u + 1):
                                    last = three(ps[:, 4 + 2 * b + u, (t % 2) * H:(t % 2 + 1) * H],
                                                 [lambda k, h=h: h[:, 1, b, k, t * P:(t + 1) * P]
                                                  for h in (hid_h, hid_l)],
                                                 [lambda k, w=w: w[:, s, 2 + b, k, :] for w in (wx_h, wx_l)])
                                last.then_inc(l3_mm, 1)

        @block.scalar
        def _(act):
            act.wait_ge(cols_in, 16)
            nc.scalar.activation(sig, cs[:, C_COND:C_COND + 4], ACT.Exp, scale=-1.0).then_inc(sig_done, 1)
            act.wait_ge(const_in, CONSTS)

            def root(nth, b):
                act.wait_ge(var_ready, nth + 1)
                nc.scalar.activation(std[b], var[b], ACT.Sqrt).then_inc(std_ready, 1)

            def transposed(c, b):
                act.wait_ge(xt_mm, c * B + (b + 1))
                for k in range(KC):
                    nc.scalar.activation(xn_t[:, b, k, :], ps[:, k, :], ACT.Identity,
                                         scale=cs[:, C_LNG + k:C_LNG + k + 1],
                                         bias=cs[:, C_LNB + k:C_LNB + k + 1]).then_inc(xn_ready, 1)

            def projected(c, b, first):
                if not first:
                    act.wait_ge(parts_out[b], c * (16 * 4))
                for o in range(4):
                    act.wait_ge(qk_mm, c * (4 * B) + (4 * b + o + 1))
                    if not (first and b == 0):
                        act.wait_ge(rest_ready, c * (4 * B) + (4 * b + o - 3))
                    bias = cs[:, C_BQK + o:C_BQK + o + 1]
                    nc.scalar.activation(qk_f[:, o, :], ps[:, 2 + o, :], ACT.Identity, bias=bias)
                    nc.scalar.activation(parts[:, b, o, 0, :], ps[:, 2 + o, :], ACT.Identity,
                                         bias=bias).then_inc(part1_ready, 1)

            def pair(c, first, last):
                nth = c * (2 * B) + 2 * B
                transposed(c, 0)
                transposed(c, 1)
                for b in range(B):
                    if not last:
                        root(nth + b, b)
                for b in range(B):
                    projected(c, b, first)
                    if not last:
                        root(nth + (B + b), b)

            for n in range(2 * B):
                root(n, n % B)
            pair(0, True, False)
            with act.Fori(1, CHUNKS - 1) as c:
                pair(c, False, False)
            pair(CHUNKS - 1, False, True)

            def acc_copy(n, par):
                act.wait_ge(pv_mm, (n + 1) * QUADS)
                nc.scalar.activation(acc_sb[:, par, :], acc_ps, ACT.Copy).then_inc(acc_out, 1)

            def m_copy(n, par, fresh, in_place):
                if not fresh:
                    act.wait_ge(m_in[par], in_place)
                act.wait_ge(mt_mm, n + 1)
                nc.scalar.activation(mrows[par][:, :], mt_ps, ACT.Copy).then_inc(mt_copied, 1)

            def steps(i, first, last):
                for s in range(2):
                    for c in range(CHUNKS):
                        n = i * (2 * CHUNKS) + (s * CHUNKS + c)
                        step0 = first and s == 0 and c == 0
                        for k in range(STILES):
                            if k % 4 == 0 and not step0:
                                act.wait_ge(pv_mm, (n - 1) * QUADS + (k // 4 + 1))
                            act.wait_ge(st_mm, n * STILES + (k + 1))
                            nc.scalar.activation(prob[:, k, :], ps[:, ST + RING[k], :], ACT.Exp,
                                                 scale=HD ** -0.5).then_inc(exp_done, 1)
                            if k == 4 and not step0:
                                if not (first and s == 0 and c < 3):
                                    act.wait_ge(ctx_mm, n - 2)
                                acc_copy(n - 1, (c + 1) % 2)
                            if k == 9 and not (last and s == 1 and c == CHUNKS - 1):
                                par = (c + 1) % 2
                                m_copy(n + 1, par, step0, (i * CHUNKS + (s * CHUNKS + c + 1 - par) // 2)
                                       * (PARTS * 16))

            for b in range(B):
                act.wait_ge(parts_out[b], 16 * 4 * CHUNKS)
            m_copy(0, 0, True, 0)
            steps(0, True, False)
            with act.Fori(1, HEADROWS // 2 - 1) as i:
                steps(i, False, False)
            steps(HEADROWS // 2 - 1, False, True)
            act.wait_ge(ctx_mm, STEPS - 2)
            acc_copy(STEPS - 1, 1)

            act.wait_ge(ctx_done, STEPS)

            def front(c):
                for b in range(B):
                    if not (isinstance(c, int) and c == 0):
                        wait_apart(act, ct_mm, (c - 1) * B + (b + 1))
                    nc.scalar.activation(c_tile[b].rearrange("p t (h d) -> p h t d", d=HD),
                                         ctx_h[:, b, :, ds(c * TILES, TILES), :], ACT.Copy).then_inc(c_copied, 1)
                for b in range(B):
                    act.wait_ge(ct_mm, c * B + (b + 1))
                    if not (isinstance(c, int) and c < 2):
                        act.wait_ge(gate_mm, (c - 2) * B + (b + 1))
                        act.wait_ge(ht_low, (c - 2) * (B * KC) + KC * (b + 1))
                    for k in range(KC):
                        nc.scalar.activation(ctx_t[b][:, k, :], ps[:, k, :], ACT.Copy).then_inc(ct_ready, 1)

            def back(c):
                for b in range(B):
                    act.wait_ge(var_ready, c * B + (2 * B * CHUNKS + b + 1))
                    nc.scalar.activation(std[b], var[b], ACT.Sqrt).then_inc(std_ready, 1)
                for b in range(B):
                    wait_apart(act, ht_mm, c * B + (b + 1))
                    for k in range(KC):
                        args = dict(bias=modc[:, 0, k, b:b + 1], scale=modc[:, 1, k, b:b + 1])
                        nc.scalar.activation(ht_h[:, k, b, ds(c * CHUNK, CHUNK)], ps[:, 6 + k, :],
                                             ACT.Identity, **args)
                        nc.scalar.activation(hc_t[b][:, k, :], ps[:, 6 + k, :], ACT.Identity,
                                             **args).then_inc(ht_ready, 1)

            front(0)
            front(1)
            back(0)
            with act.Fori(1, CHUNKS - 1) as c:
                front(c + 1)
                back(c)
            back(CHUNKS - 1)
            act.wait_ge(logits_less, 1)
            nc.scalar.activation(gate_p, gate_p, ACT.Exp).then_inc(gate_exp, 1)
            for m in range(B * CHUNKS):
                act.wait_ge(cwt_mm, m + 1)
                if m >= 2:
                    act.wait_ge(b3_mm, m - 1)
                nc.scalar.activation(cwt[m % 2], ps[0:EXPERTS, 6 + m % 2, :], ACT.Copy).then_inc(cwt_ready, 1)

            act.wait_ge(acc_init, B * CHUNKS)
            with act.Fori(0, EXPERTS // 2) as e2:
                for s in range(2):
                    with act.Fori(0, CHUNKS) as c:
                        f = e2 * (2 * CHUNKS) + c + s * CHUNKS
                        for j in range(8):
                            l, b, fo = j // 4, j // 2 % 2, j % 2
                            bank, bias = ps[:, 2 * b + fo, :], exb[:, s, KC * l + fo:KC * l + fo + 1]
                            act.wait_ge(h_mm, f * 8 + (j + 1))
                            nc.scalar.activation(hid_h[:, l, b, fo, :], bank, ACT.Relu, bias=bias)
                            act.wait_ge(low_out, f * 8 + (j + 1))
                            nc.scalar.activation(h_full[:, j % 2, :], bank, ACT.Relu,
                                                 bias=bias).then_inc(relu_out, 1)

        @block.vector
        def _(dve):
            v = nc.vector
            count = [0]

            def step(ins):
                ins.then_inc(dve_step, 1)
                count[0] += 1
                dve.wait_ge(dve_step, count[0])

            v.memset(vs[:, :, :, :], 0.0).then_inc(dve_step, 1)
            v.memset(k6[96:128, :, :], 1.0)
            dve.wait_ge(dve_step, 1)
            count[0] = 1
            v.memset(vs[:, :, :, HD:HD + 1], 1.0).then_inc(fixed_done, 1)
            dve.wait_ge(cols_in, 16)
            dve.wait_ge(sig_done, 1)
            step(v.tensor_scalar(mneg, sig, 1.0, None, ALU.add))
            step(v.reciprocal(mres, mneg))
            step(v.tensor_tensor(silu, mres, cs[:, C_COND:C_COND + 4], ALU.mult))
            for k in range(KC):
                v.tensor_copy(cond_b[:, k], silu[:, k * B:(k + 1) * B].unsqueeze(2).to_broadcast([P, B, P])
                              ).then_inc(cond_done, 1)
            LN = 7

            def normalise(src, b, at, nth):
                for t in range(TILES):
                    last = v.bn_stats(stats[b][:, t, :], src(t))
                last.then_inc(dve_step, 1)
                wait_apart(dve, dve_step, at + 1)
                for t in range(TILES):
                    last = v.bn_aggr(mv[b][:, t, :], stats[b][:, t, :])
                last.then_inc(dve_step, 1)
                dve.wait_ge(dve_step, at + 2)
                v.tensor_scalar(var[b], mv[b][:, :, 1], EPS, None, ALU.add).then_inc(var_ready, 1)
                dve.wait_ge(std_ready, nth + 1)
                v.reciprocal(rstd[b], std[b]).then_inc(dve_step, 1)
                dve.wait_ge(dve_step, at + 3)
                v.tensor_tensor(std[b], rstd[b], rstd[b], ALU.mult).then_inc(dve_step, 1)
                dve.wait_ge(dve_step, at + 4)
                v.tensor_tensor(std[b], std[b], var[b], ALU.mult).then_inc(dve_step, 1)
                dve.wait_ge(dve_step, at + 5)
                v.tensor_scalar(std[b], std[b], -0.5, 1.5, ALU.mult, ALU.add).then_inc(dve_step, 1)
                dve.wait_ge(dve_step, at + 6)
                v.tensor_tensor(rstd[b], rstd[b], std[b], ALU.mult).then_inc(dve_step, 1)
                dve.wait_ge(dve_step, at + 7)

            def centred(dst, src, b, t):
                return v.tensor_scalar(dst, src, mv[b][:, t, 0:1], rstd[b][:, t:t + 1], ALU.subtract, ALU.mult)

            def x_tile(b, t):
                return xs[:, b, ds(t, 1), :].rearrange("p t f -> p (t f)")

            def first_norm(c, b, at):
                normalise(lambda t: x_tile(b, c * TILES + t), b, at, c * (2 * B) + b)
                v.tensor_copy(mean1[:, b, ds(c * TILES, TILES)], mv[b][:, :, 0])
                v.tensor_copy(rstd1[:, b, ds(c * TILES, TILES)], rstd[b])
                for t in range(TILES):
                    last = centred(h_tile[:, b, t, :], x_tile(b, c * TILES + t), b, t)
                last.then_inc(ln1_done, 1)

            def second_norm(c, b, at):
                wait_apart(dve, h_ready, c * B + (b + 1))
                normalise(lambda t: h_tile[:, b, t, :], b, at, c * (2 * B) + (B + b))
                for t in range(TILES):
                    last = centred(y_tile[:, b, t, :], h_tile[:, b, t, :], b, t)
                last.then_inc(y_ready, 1)

            def split(c, b, at):
                for o in range(4):
                    dve.wait_ge(rest_ready, c * (4 * B) + (4 * b + o + 1))
                    v.tensor_copy(parts[:, b, o, 1, :], rest[:, o % 2, :]).then_inc(dve_step, 1)
                    dve.wait_ge(dve_step, at + o + 1)
                    v.tensor_tensor(parts[:, b, o, 2, :], rest[:, o % 2, :], parts[:, b, o, 1, :],
                                    ALU.subtract).then_inc(parts_ready, 1)
                for u in range(2):
                    dve.wait_ge(v_mm, c * (2 * B) + (2 * b + u + 1))
                    v.tensor_tensor(
                        v_heads[:, b * HEADS:(b + 1) * HEADS, ds(c * TILES + 2 * u, 2), :].rearrange(
                            "p h t d -> p t h d"),
                        ps[:, 6 + u, :].rearrange("p (t h d) -> p t h d", t=2, d=HD),
                        on_two(rs[:, R_BV:R_BV + H], 2).rearrange("p t (h d) -> p t h d", d=HD),
                        ALU.add).then_inc(v_ready, 1)

            NORMS, SPLITS = 2 * B * LN, B * 4

            def pair(c, at, last):
                if not last:
                    for b in range(B):
                        first_norm(c + 1, b, at + b * LN)
                at += 0 if last else B * LN
                for b in range(B):
                    split(c, b, at)
                    at += 4
                    if not last:
                        second_norm(c + 1, b, at)
                        at += LN

            dve.wait_ge(x_in[0], 16 * B)
            base = count[0]
            for b in range(B):
                first_norm(0, b, base + b * LN)
            count[0] = base + B * LN
            dve.wait_ge(mod_mm, 1)
            dve.wait_ge(const_in, CONSTS)
            for b in range(B):
                def blk(i):
                    return ps[:, 3 * b + i // 2, (i % 2) * H:(i % 2 + 1) * H]
                v.tensor_scalar(mod[:, b, M_CA], blk(CA), 1.0, None, ALU.add)
                v.tensor_copy(mod[:, b, M_SA], blk(SA))
                for m, i in ((M_GA, GA), (M_GB, GB)):
                    v.tensor_scalar(gtmp[:, 0], blk(i), 0.0, 2.0, ALU.is_ge, ALU.mult)
                    step(v.tensor_scalar(gtmp[:, 1], blk(i), -1.0, FLOOR, ALU.mult, ALU.max))
                    step(v.tensor_tensor(gtmp[:, 1], blk(i), gtmp[:, 1], ALU.max))
                    step(v.scalar_tensor_tensor(mod[:, b, m], gtmp[:, 0], -1.0, gtmp[:, 1], ALU.add, ALU.mult))
                v.tensor_tensor(gah[:, b, 0], mod[:, b, M_GA], mod[:, b, M_CA], ALU.mult)
                step(v.tensor_tensor(gtmp[:, 0], mod[:, b, M_SA], rs[:, R_BO:R_BO + H], ALU.add))
                step(v.tensor_tensor(gah[:, b, 1], gtmp[:, 0], mod[:, b, M_GA], ALU.mult))
                v.tensor_tensor(b3g[:, b], b3s[:, :], mod[0:EXPERTS, b, M_GB], ALU.mult)
            cview = ps[:, 6, 0:2 * KC * B].rearrange("p (m k b) -> p m k b", m=2, k=KC)
            v.tensor_copy(modc[:, 0], cview[:, 0])
            v.tensor_scalar(modc[:, 1], cview[:, 1], 1.0, None, ALU.add).then_inc(mod_done, 1)
            dve.wait_ge(mod_done, 1)

            dve.wait_ge(x_in[1], 16 * B * (CHUNKS - 1))
            base = count[0]
            for b in range(B):
                second_norm(0, b, base + b * LN)
            base += B * LN
            with dve.Fori(0, CHUNKS - 1) as c:
                pair(c, c * (NORMS + SPLITS) + base, False)
            base += (NORMS + SPLITS) * (CHUNKS - 1)
            pair(CHUNKS - 1, base, True)
            base += SPLITS

            def maximum(n, par, o):
                dve.wait_ge(scores_mm, n * OPS + (o + 1))
                if o == 0 and not (isinstance(n, int) and n < 2):
                    dve.wait_ge(top_done, n - 1)
                v.tensor_reduce(mx[par][:, o // 4, o % 4:o % 4 + 1], ps[:, SCORE + RING[o], :],
                                AX.X, ALU.max).then_inc(max_done, 1)

            def top(n, par, fresh):
                dve.wait_ge(max_done, (n + 1) * OPS)
                if not fresh:
                    dve.wait_ge(m_parts, n - 1)
                v.tensor_reduce(mtop[par], mx[par], AX.X, ALU.max).then_inc(top_done, 1)

            def context_sum(n, par):
                dve.wait_ge(ctx_mm, n + 1)
                if not (isinstance(n, int) and n < 2):
                    dve.wait_ge(ctx_done, n - 1)
                v.tensor_reduce(ctx_sum[par], ctx_ps[:, :, :, 0:HD + 1].rearrange("p t g n -> p t n g"),
                                AX.X, ALU.add).then_inc(ctx_read, 1)

            def context_rec(n, par):
                dve.wait_ge(ctx_read, n + 1)
                v.reciprocal(rec[par], ctx_sum[par][:, :, HD]).then_inc(rec_ready, 1)

            def steps(i, first, last):
                for s in range(2):
                    for c in range(CHUNKS):
                        n = i * (2 * CHUNKS) + (s * CHUNKS + c)
                        for o in range(OPS):
                            if not (last and s == 1 and c >= 2):
                                maximum(n + 2, c % 2, o)
                            if o == 1 and not (last and s == 1 and c == CHUNKS - 1):
                                top(n + 1, (c + 1) % 2, first and s == 0 and c == 0)
                            if not (first and s == 0 and c < 2):
                                if o == 3:
                                    context_sum(n - 2, c % 2)
                                elif o == 5:
                                    context_rec(n - 2, c % 2)

            for n in range(2):
                for o in range(OPS):
                    maximum(n, n, o)
                if n == 0:
                    top(0, 0, True)
            steps(0, True, False)
            with dve.Fori(1, HEADROWS // 2 - 1) as i:
                steps(i, False, False)
            steps(HEADROWS // 2 - 1, False, True)
            for n in (STEPS - 2, STEPS - 1):
                context_sum(n, n % 2)
                context_rec(n, n % 2)

            def proj_add(c, b, at):
                dve.wait_ge(proj_mm, c * B + (b + 1))
                for u in range(2):
                    last = v.tensor_tensor(z_tile[b][:, 2 * u:2 * u + 2, :],
                                           ps[:, 2 + 2 * b + u, :].rearrange("p (t f) -> p t f", f=H),
                                           on_two(mod[:, b, M_GA], 2), ALU.mult)
                last.then_inc(proj_read, 1)
                dve.wait_ge(proj_read, c * B + (b + 1))
                xt = xs[:, b, ds(c * TILES, TILES), :]
                v.tensor_tensor(xt, xt, z_tile[b], ALU.add).then_inc(dve_step, 1)
                wait_apart(dve, dve_step, at + 1)
                normalise(lambda t: x_tile(b, c * TILES + t), b, at + 1, c * B + (2 * B * CHUNKS + b))
                for t in range(TILES):
                    last = centred(z_tile[b][:, t, :], x_tile(b, c * TILES + t), b, t)
                last.then_inc(z_ready, 1)

            per = B * (1 + LN)
            dve.wait_ge(xr_done, HEADROWS // 2)
            with dve.Fori(0, CHUNKS) as c:
                for b in range(B):
                    proj_add(c, b, c * per + (base + b * (1 + LN)))
                for b in range(B):
                    for k in range(KC):
                        dve.wait_ge(ht_ready, c * (B * KC) + (b * KC + k + 1))
                        t = ds(c * CHUNK, CHUNK)
                        v.tensor_tensor(ht_l[:, k, b, t], hc_t[b][:, k, :], ht_h[:, k, b, t].bitcast(f32),
                                        ALU.subtract).then_inc(ht_low, 1)
                for b in range(B):
                    dve.wait_ge(gate_mm, c * B + (b + 1))
                    v.tensor_tensor(logits[:, b, ds(c * TILES, TILES), :],
                                    ps[:, b, 0:TILES * EXPERTS].rearrange("p (t e) -> p t e", e=EXPERTS),
                                    on_two(rs[:, R_GB:R_GB + EXPERTS], TILES), ALU.add).then_inc(gl_read, 1)
            base += per * CHUNKS

            count[0] = base
            NT = B * STILES
            wide = [P, NT, EXPERTS]

            def over(a):
                return a.unsqueeze(2).to_broadcast(wide)

            iota = on_two(cs[:, C_IOTA:C_IOTA + EXPERTS], NT)
            left, where, one, two = gate_t5
            top, at_top, total, inv = gate_s
            dve.wait_ge(gl_read, B * CHUNKS)
            step(v.tensor_reduce(top, gate_p, AX.X, ALU.max))
            v.tensor_tensor(gate_p, gate_p, over(top), ALU.subtract).then_inc(logits_less, 1)
            dve.wait_ge(gate_exp, 1)
            step(v.tensor_reduce(total, gate_p, AX.X, ALU.add))
            step(v.reciprocal(inv, total))
            step(v.tensor_tensor(left, gate_p, over(inv), ALU.mult))
            step(v.tensor_copy(gate_p, left))
            for chosen in (one, two):
                step(v.tensor_reduce(top, left, AX.X, ALU.max))
                step(v.tensor_tensor(where, left, over(top), ALU.is_lt))
                step(v.scalar_tensor_tensor(where, where, float(EXPERTS), iota, ALU.mult, ALU.add))
                step(v.tensor_reduce(at_top, where, AX.X, ALU.min))
                step(v.tensor_tensor(chosen, iota, over(at_top), ALU.is_equal))
                if chosen is one:
                    step(v.scalar_tensor_tensor(left, one, -2.0, left, ALU.mult, ALU.add))
            v.tensor_tensor(one, one, gate_p[:, :, 0:1].to_broadcast(wide), ALU.mult)
            step(v.tensor_tensor(two, two, gate_p[:, :, 1:2].to_broadcast(wide), ALU.mult))
            v.tensor_tensor(cw[:, :, :, :].rearrange("p b t e -> p (b t) e"), one, two,
                            ALU.add).then_inc(cw_done, 1)
            for m in range(B * CHUNKS):
                b, c = m // CHUNKS, m % CHUNKS
                dve.wait_ge(b3_mm, m + 1)
                for u in range(2):
                    xt = xs[:, b, c * TILES + 2 * u:c * TILES + 2 * u + 2, :]
                    last = v.tensor_tensor(xt, xt, ps[:, 2 + 2 * (m % 2) + u, :].rearrange(
                        "p (t f) -> p t f", f=H), ALU.add)
                last.then_inc(acc_init, 1)

            dve.wait_ge(acc_init, B * CHUNKS)
            v.memset(free_at_first[:, 0:1], 0.0).then_inc(relu_out, 4)
            v.memset(free_at_first[:, 1:2], 0.0).then_inc(l3_out, 4)
            v.memset(free_at_first[:, 2:3], 0.0).then_inc(low_out, 2)
            with dve.Fori(0, EXPERTS // 2) as e2:
                for s in range(2):
                    with dve.Fori(0, CHUNKS) as c:
                        f = e2 * (2 * CHUNKS) + c + s * CHUNKS
                        for j in range(8):
                            l, b, fo = j // 4, j // 2 % 2, j % 2
                            dve.wait_ge(relu_out, f * 8 + (4 + j + 1))
                            v.tensor_tensor(hid_l[:, l, b, fo, :], h_full[:, j % 2, :],
                                            hid_h[:, l, b, fo, :].bitcast(f32), ALU.subtract).then_inc(low_out, 1)
                        for b in range(B):
                            for u in range(2):
                                dve.wait_ge(l3_mm, f * 4 + (2 * b + u + 1))
                                for t in (2 * u, 2 * u + 1):
                                    tile = xs[:, b, ds(c * TILES + t, 1), :].rearrange("p t f -> p (t f)")
                                    w = cw[:, b, ds(c * TILES + t, 1), ds(e2 * 2 + s, 1)].rearrange(
                                        "p t e -> p (t e)")
                                    last = v.scalar_tensor_tensor(
                                        tile, ps[:, 4 + 2 * b + u, (t % 2) * H:(t % 2 + 1) * H], w, tile,
                                        ALU.mult, ALU.add)
                                last.then_inc(l3_out, 1)

        @block.gpsimd
        def _(pool):
            g = nc.gpsimd
            pool.wait_ge(mod_done, 1)
            def modulate(c, b, at):
                h = h_tile[:, b]
                pool.wait_ge(ln1_done, c * B + (b + 1))
                g.tensor_tensor(h, h, on_two(mod[:, b, M_CA], TILES), ALU.mult).then_inc(pool_step, 1)
                pool.wait_ge(pool_step, at + 1)
                g.tensor_tensor(h, h, on_two(mod[:, b, M_SA], TILES), ALU.add).then_inc(h_ready, 1)

            def leave(c, b, first):
                for o in range(4):
                    if not (first and b == 0 and o < 2):
                        pool.wait_ge(parts_ready, c * (4 * B) + (4 * b + o - 1))
                    pool.wait_ge(part1_ready, c * (4 * B) + (4 * b + o + 1))
                    g.tensor_tensor(rest[:, o % 2, :], qk_f[:, o, :], parts[:, b, o, 0, :],
                                    ALU.subtract).then_inc(rest_ready, 1)

            def pair(c, first, last):
                for b in range(B):
                    if not last:
                        modulate(c + 1, b, c * B + (B + b))
                    leave(c, b, first)

            for b in range(B):
                modulate(0, b, b)
            pair(0, True, False)
            with pool.Fori(1, CHUNKS - 1) as c:
                pair(c, False, False)
            pair(CHUNKS - 1, False, True)
            base = B * CHUNKS

            def stage_v(gi, s):
                g.tensor_copy(vs[:, s, :, 0:HD], v_heads[:, ds(gi, 1), :, :].rearrange(
                    "p g t d -> p (g t) d")).then_inc(v_staged, 1)

            def residual(i):
                for b in range(B):
                    x_t = xs[:, b, ds(i * 1, 1), :].rearrange("p t f -> p (t f)")
                    r = xr[:, b]
                    wide = [P, H]
                    chain = ((r, x_t, mean1[:, b, ds(i * 1, 1)].to_broadcast(wide), ALU.subtract),
                             (r, r, rstd1[:, b, ds(i * 1, 1)].to_broadcast(wide), ALU.mult),
                             (r, r, gah[:, b, 0], ALU.mult), (r, r, gah[:, b, 1], ALU.add))
                    for n, (o, a0, a1, op) in enumerate(chain):
                        g.tensor_tensor(o, a0, a1, op).then_inc(xr_step, 1)
                        wait_apart(pool, xr_step, i * (4 * B) + (4 * b + n + 1))
                    ins = g.tensor_tensor(x_t, x_t, r, ALU.add)
                ins.then_inc(xr_done, 1)

            STEP = 5

            def m_prepare(n, par, fresh):
                at = n * STEP + base
                if not fresh:
                    pool.wait_ge(mt_mm, n - 1)
                wait_apart(pool, top_done, n + 1)
                pa = mparts[par]
                g.tensor_scalar(mneg, mtop[par], -1.0, None, ALU.mult).then_inc(pool_step, 1)
                wait_apart(pool, pool_step, at + 1)
                g.tensor_copy(pa[:, 0, :], mneg).then_inc(pool_step, 1)
                pool.wait_ge(pool_step, at + 2)
                g.tensor_tensor(mres, mneg, pa[:, 0, :], ALU.subtract).then_inc(pool_step, 1)
                wait_apart(pool, pool_step, at + 3)
                g.tensor_copy(pa[:, 1, :], mres).then_inc(pool_step, 1)
                pool.wait_ge(pool_step, at + 4)
                g.tensor_tensor(mres2, mres, pa[:, 1, :], ALU.subtract).then_inc(pool_step, 1)
                wait_apart(pool, pool_step, at + 5)
                g.tensor_copy(pa[:, 2, :], mres2).then_inc(m_parts, 1)

            def context(n, par):
                wait_apart(pool, rec_ready, n + 1)
                g.tensor_tensor(ctx_q[:, ds(n * TILES, TILES), :], ctx_sum[par][:, :, 0:HD],
                                rec[par].unsqueeze(2).to_broadcast([P, TILES, HD]),
                                ALU.mult).then_inc(ctx_done, 1)

            def steps(i, first, last):
                for s in range(2):
                    for c in range(CHUNKS):
                        n = i * (2 * CHUNKS) + (s * CHUNKS + c)
                        if c == 1 and not (last and s == 1):
                            if not (first and s == 0):
                                wait_apart(pool, pv_mm, (i * 2 + s) * (CHUNKS * QUADS))
                            stage_v(i * 2 + (s + 1), 1 - s)
                        if not (last and s == 1 and c == CHUNKS - 1):
                            m_prepare(n + 1, (c + 1) % 2, first and s == 0 and c == 0)
                        if not (first and s == 0 and c < 2):
                            context(n - 2, c % 2)
                        if s == 0 and c == 2:
                            residual(i)

            pool.wait_ge(v_ready, 2 * B * CHUNKS)
            pool.wait_ge(fixed_done, 1)
            stage_v(0, 0)
            m_prepare(0, 0, True)
            steps(0, True, False)
            with pool.Fori(1, HEADROWS // 2 - 1) as i:
                steps(i, False, False)
            steps(HEADROWS // 2 - 1, False, True)
            for n in (STEPS - 2, STEPS - 1):
                context(n, n % 2)

            def split_expert(e, s, at):
                if not (isinstance(e, int) and e < 2):
                    wait_apart(pool, l3_mm, (e - 1) * (4 * CHUNKS))
                wait_apart(pool, raw_in, (e + 1) * (3 * 16))
                g.tensor_copy(exb[:, s, :], cs[:, ds(C_EB + e * (2 * KC), 2 * KC)])
                n = 0
                for slot in range(2):
                    g.tensor_copy(wx_h[:, s, slot], raw[:, slot]).then_inc(w_step, 1)
                    wait_apart(pool, w_step, at + (n + 1))
                    g.tensor_tensor(wx_l[:, s, slot], raw[:, slot], wx_h[:, s, slot].bitcast(f32),
                                    ALU.subtract).then_inc(w_step, 1)
                    n += 2
                for b in range(B):
                    pool.wait_ge(w_step, at + n)
                    g.tensor_tensor(w3g, raw[:, 2], on_two(mod[:, b, M_GB], KC), ALU.mult).then_inc(w_step, 1)
                    wait_apart(pool, w_step, at + (n + 1))
                    g.tensor_copy(wx_h[:, s, 2 + b], w3g).then_inc(w_step, 1)
                    pool.wait_ge(w_step, at + (n + 2))
                    g.tensor_tensor(wx_l[:, s, 2 + b], w3g, wx_h[:, s, 2 + b].bitcast(f32),
                                    ALU.subtract).then_inc(w_split if b else w_step, 1)
                    n += 3

            PER = 9
            pool.wait_ge(ctx_done, STEPS)
            pool.wait_ge(acc_init, B * CHUNKS)
            for e in range(2):
                split_expert(e, e, e * PER)
            with pool.Fori(1, EXPERTS // 2) as e2:
                for s in range(2):
                    split_expert(e2 * 2 + s, s, e2 * (2 * PER) + s * PER)


def kernel(**inputs):
    import ml_dtypes
    import numpy as np
    from concourse import bacc
    from concourse.bass_utils import run_bass_kernel_spmd

    a = {n.replace("L0_", ""): np.asarray(v) for n, v in inputs.items()}

    def columns(v):
        return v.reshape(-1, KC, P).transpose(2, 0, 1).reshape(P, -1)

    def repeated(v):
        return np.broadcast_to(v.reshape(1, -1), (P, v.size))

    cond = a["c"].reshape(B, KC, P).transpose(2, 1, 0).reshape(P, KC * B)
    cols = np.concatenate([cond, columns(a["attn_b_qkv"][:2 * H]), columns(a["attn_ln_gamma"]),
                           columns(a["attn_ln_beta"]), columns(np.stack([a["ffn_b1"], a["ffn_b2"]], axis=1)),
                           repeated(np.arange(EXPERTS, dtype=np.float32))], axis=1)
    rows = np.concatenate([repeated(a["attn_b_qkv"][2 * H:]), repeated(a["attn_b_out"]),
                           repeated(a["ffn_gate_b"])], axis=1)
    eye = np.eye(P, dtype=np.float32)
    arrays = {
        "x": a["attn_hidden_states"], "cols": cols, "rows": rows, "wmod": a["wmod"],
        "wqkv_t": a["attn_W_qkv"].T, "wout_t": a["attn_W_out"].T, "gate_t": a["ffn_gate_w"].T,
        "w1": a["ffn_w1"], "w2": a["ffn_w2"], "w3": a["ffn_w3"], "b3": a["ffn_b3"],
        "ident": eye, "ident_b": eye.astype(ml_dtypes.bfloat16),
    }
    arrays = {n: np.ascontiguousarray(v) for n, v in arrays.items()}
    nc = bacc.Bacc("TRN2", target_bir_lowering=False, num_devices=1)
    aps = {n: nc.dram_tensor(n, v.shape, mybir.dt.from_np(v.dtype), kind="ExternalInput").ap()
           for n, v in arrays.items()}
    out = nc.dram_tensor("out", (B, S, H), mybir.dt.float32, kind="ExternalOutput").ap()
    build(nc, out=out, **aps)
    return run_bass_kernel_spmd(nc, [arrays], core_ids=[0]).results[0]["out"]
```

```python
import concourse.bass as bass
from concourse import mybir
from contextlib import ExitStack

P = 128
B, S, H = 2, 2048, 256
HEADS, HD = 16, 16
EXPERTS = 8
EPS = 1e-5
FLOOR = 0.25
KC = H // P
CHUNK = 512
CHUNKS = S // CHUNK
TILES = CHUNK // P
STILES = S // P
HEADROWS = B * HEADS
PARTS = 3
TERMS = 6
TROWS = TERMS * HD
HEAD_DMAS = 2 * TERMS
GW = 32
VW = 32
C_COND, C_BQK, C_LNG, C_LNB = 0, 4, 8, 10
C_EB = 12
C_IOTA = 44
NCOLS = 52
R_BV, R_BO, R_GB = 0, H, 2 * H
NROWS = 2 * H + EXPERTS
SA, CA, GA, SB_, CB, GB = range(6)
M_CA, M_SA, M_GA, M_GB = range(4)


def build(nc, x, cols, rows, wmod, wqkv_t, wout_t, gate_t, w1, w2, w3, b3, ident, ident_b, out):
    f32, f32r, bf16 = mybir.dt.float32, mybir.dt.float32r, mybir.dt.bfloat16
    ALU, ACT, AX = mybir.AluOpType, mybir.ActivationFunctionType, mybir.AxisListType
    ds = bass.ds
    ctx = ExitStack()

    def sb(name, shape, dt=f32):
        return ctx.enter_context(nc.sbuf_tensor(name, shape, dt))

    def sem(name):
        return ctx.enter_context(nc.semaphore(name))

    with ctx:
        q_parts = nc.dram_tensor("q_parts", [PARTS, HEADROWS * HD, S], bf16, kind="Internal").ap()
        k_parts = nc.dram_tensor("k_parts", [PARTS, HEADROWS * HD, S], bf16, kind="Internal").ap()

        xs = sb("xs", [P, B, STILES, H])
        cs = sb("cs", [P, NCOLS])
        rs = sb("rs", [P, NROWS])
        mod = sb("mod", [P, B, 4, H])
        gah = sb("gah", [P, B, 2, H])
        mean1 = sb("mean1", [P, B, STILES])
        rstd1 = sb("rstd1", [P, B, STILES])
        modc = sb("modc", [P, 2, KC, B])
        wout = sb("wout", [P, KC, H])
        gatew = sb("gatew", [P, KC, GW])
        raw_b3 = sb("raw_b3", [P, H])
        idf = sb("idf", [P, P])
        idb = sb("idb", [P, P], bf16)
        cw = sb("cw", [P, STILES, B, EXPERTS])
        small = sb("small", [P, 384])
        raw = sb("raw", [P, 3, KC, H])
        exb = sb("exb", [P, 2, 2 * KC])
        t3 = sb("t3", [P, 4 * TILES * H])

        at = [0]

        def piece(n):
            at[0] += n
            return small[:, at[0] - n:at[0]]

        stats = piece(B * TILES * 6).rearrange("p (t n) -> p t n", n=6)
        mv = piece(B * TILES * 2).rearrange("p (t n) -> p t n", n=2)
        rstd, var, std, nmr = (piece(B * TILES) for _ in range(4))
        mx = [piece(16).rearrange("p (t n) -> p t n", n=4) for _ in range(2)]
        silu = piece(4)
        mtop = [piece(4) for _ in range(2)]
        mneg = piece(4)
        mres = piece(4)
        mres2 = piece(4)
        sig = piece(4)
        free_at_first = piece(3)
        ctx_sum = [piece(TILES * (HD + 1)).rearrange("p (t n) -> p t n", t=TILES) for _ in range(2)]
        rec = [piece(4) for _ in range(B)]
        logits = sb("logits", [P, STILES, B, EXPERTS])
        mparts = [sb(f"mparts{n}", [P, PARTS, TILES], bf16) for n in range(2)]
        mrows = [sb(f"mrows{n}", [PARTS * TILES, P], bf16) for n in range(2)]
        b3g = sb("b3g", [P, B, H])

        early = ExitStack()

        def sb_early(name, shape, dt=f32):
            return early.enter_context(nc.sbuf_tensor(name, shape, dt))

        vall = sb_early("vall", [P, HEADROWS * STILES * HD])
        pall = sb_early("pall", [P, STILES * CHUNK])
        q6 = sb_early("q6", [P, 2, S], bf16)
        k6 = sb_early("k6", [P, 2, S], bf16)
        vs = sb_early("vs", [P, 2, STILES, VW])
        acc_sb = sb_early("acc_sb", [P, 2, CHUNK])
        xr = sb_early("xr", [P, B, H])
        wog = sb_early("wog", [P, B, KC, H])
        early.close()
        late = ExitStack()

        def sb_late(name, shape, dt=f32):
            return late.enter_context(nc.sbuf_tensor(name, shape, dt))

        ht_h = sb_late("ht_h", [P, KC, B, S], f32r)
        ht_l = sb_late("ht_l", [P, KC, B, S], f32r)
        wx_h = sb_late("wx_h", [P, 2, 4, KC, H], f32r)
        wx_l = sb_late("wx_l", [P, 2, 4, KC, H], f32r)
        with nc.sbuf_tensor("call", [P, HEADROWS * STILES * HD], f32) as call:
            pass
        hid_h = sb_late("hid_h", [P, 2, B, KC, CHUNK], f32r)
        hid_l = sb_late("hid_l", [P, 2, B, KC, CHUNK], f32r)
        late.close()

        v_heads = vall[:, :].rearrange("p (g t d) -> p g t d", t=STILES, d=HD)
        ctx_q = call[:, :].rearrange("p (n d) -> p n d", d=HD)
        ctx_h = call[:, :].rearrange("p (b h t d) -> p b h t d", b=B, h=HEADS, d=HD)
        s1 = call[:, :].rearrange("p (u b n) -> p u b n", u=4, b=B)
        h_tile = s1[:, 0].rearrange("p b (t f) -> p b t f", f=H)
        y_tile = s1[:, 1].rearrange("p b (t f) -> p b t f", f=H)
        xn_t = s1[:, 2].rearrange("p b (k s) -> p b k s", k=KC)
        wm = call[:, 4096:4096 + KC * 6 * H].rearrange("p (k n) -> p k n", k=KC)
        qk_f = pall[:, 0:4 * CHUNK].rearrange("p (o s) -> p o s", o=4)
        parts = pall[:, 4 * CHUNK:].bitcast(bf16).rearrange("p (b o r s) -> p b o r s", b=B, o=4, r=PARTS)
        rest = [acc_sb[:, 0], acc_sb[:, 1]] + [wog[:, n].rearrange("p k f -> p (k f)") for n in range(2)]
        rest_v = t3[:, 4 * TILES * H - CHUNK:]
        prob = pall[:, :].rearrange("p (k s) -> p k s", s=CHUNK)
        t3v = t3[:, :].rearrange("p (u n) -> p u n", u=4)
        k6f = k6[:, :, :].bitcast(f32)
        wqkv = t3[:, 2 * TILES * H:2 * TILES * H + KC * 3 * H].rearrange("p (k n) -> p k n", k=KC)
        c_tile = [k6f[:, b].rearrange("p (t f) -> p t f", f=H) for b in range(B)]
        z_tile = [t3v[:, b].rearrange("p (t f) -> p t f", f=H) for b in range(B)]
        hc_t = ctx_t = [t3v[:, 2 + b].rearrange("p (k s) -> p k s", k=KC) for b in range(B)]
        h_full = t3v[:, 0].rearrange("p (n s) -> p n s", n=2)
        cond_b = t3v[:, 0, 0:KC * B * P].rearrange("p (k b n) -> p k b n", k=KC, b=B)
        gtmp = t3v[:, 1].rearrange("p (a n) -> p a n", a=2)
        gate_sb = xr[:, :, :].rearrange("p b f -> p (b f)")
        GATES = STILES * B * EXPERTS
        gate_mem = k6f[:, :, :].rearrange("p b n -> p (b n)")
        gate_wide = [gate_mem[:, n * GATES:(n + 1) * GATES].rearrange("p (t e) -> p t e", e=EXPERTS) for n in range(4)]
        gate_slim = [gate_mem[:, 4 * GATES + n * STILES * B:4 * GATES + (n + 1) * STILES * B] for n in range(4)]
        gate_p = logits[:, :, :, :].rearrange("p t b e -> p (t b) e")
        gate_w = cw[:, :, :, :].rearrange("p t b e -> p (t b) e")
        GATE_PARTS = [slice(0, (CHUNKS - 1) * TILES * B), slice((CHUNKS - 1) * TILES * B, STILES * B)]
        w3g = gah[:, 0, :, :]
        b3x = [b3g[:, :, :], gah[:, 1, :, :]]

        ps = ctx.enter_context(nc.psum_tensor("ps", [P, 8, CHUNK], f32))
        TB = (0, 6)
        gl_ps = ps[:, 7, :].rearrange("p (t b k e) -> p t b k e", t=TILES, b=B, k=KC)
        MISC, ACC = 7, 6
        RING = [0, 1, 2, 0, 1, 2, 0, 1, 0, 2, 1, 0, 2, 1, 0, 2]
        BACK = [next(d for d in range(1, 17) if RING[u - d] == RING[u]) for u in range(16)]
        SCORE, ST = 0, 3
        acc_ps = ps[:, ACC, :]
        ctx_ps = ps[:, MISC, :].rearrange("p (t g n) -> p t g n", t=TILES, g=4)
        mt_ps = ps[0:PARTS * TILES, MISC, 0:P // 2].bitcast(bf16)

        cols_in = sem("cols_in")
        const_in = sem("const_in")
        x_in = [sem(f"x_in{n}") for n in range(2)]
        wmod_in = [sem(f"wmod_in{n}") for n in range(2)]
        sig_done = sem("sig_done")
        cond_done = sem("cond_done")
        ca_mm = sem("ca_mm")
        mod_mm = sem("mod_mm")
        gates_done = sem("gates_done")
        fills = sem("fills")
        fixed_done = sem("fixed_done")
        dve_step = sem("dve_step")
        pool_step = sem("pool_step")
        var_ready = sem("var_ready")
        std_ready = sem("std_ready")
        ln1_done = sem("ln1_done")
        h_ready = sem("h_ready")
        h_first = sem("h_first")
        xr_step = sem("xr_step")
        xr_done = sem("xr_done")
        rest_ready = sem("rest_ready")
        rest_own = sem("rest_own")
        ca_ready = sem("ca_ready")
        ga_copied = sem("ga_copied")
        nmr_ready = sem("nmr_ready")
        y_ready = sem("y_ready")
        xt_mm = sem("xt_mm")
        xn_ready = sem("xn_ready")
        qk_mm = sem("qk_mm")
        v_mm = sem("v_mm")
        part1_ready = sem("part1_ready")
        parts_ready = sem("parts_ready")
        v_ready = sem("v_ready")
        parts_out = [sem(f"parts_out{b}") for b in range(B)]
        head_in = [sem(f"head_in{s}") for s in range(2)]
        v_staged = sem("v_staged")
        scores_mm = sem("scores_mm")
        max_done = sem("max_done")
        top_done = sem("top_done")
        m_parts = sem("m_parts")
        mt_mm = sem("mt_mm")
        mt_copied = sem("mt_copied")
        m_in = [sem(f"m_in{s}") for s in range(2)]
        st_mm = sem("st_mm")
        exp_done = sem("exp_done")
        pv_mm = sem("pv_mm")
        acc_out = sem("acc_out")
        ctx_mm = sem("ctx_mm")
        ctx_read = sem("ctx_read")
        rec_ready = sem("rec_ready")
        ctx_done = sem("ctx_done")
        c_copied = sem("c_copied")
        ct_mm = sem("ct_mm")
        ct_ready = sem("ct_ready")
        proj_mm = sem("proj_mm")
        proj_read = sem("proj_read")
        z_ready = sem("z_ready")
        ht_mm = sem("ht_mm")
        ht_ready = sem("ht_ready")
        gate_mm = sem("gate_mm")
        gl_copied = sem("gl_copied")
        gl_mm = sem("gl_mm")
        gl_summed = sem("gl_summed")
        gl_read = sem("gl_read")
        logits_less = sem("logits_less")
        gate_exp = sem("gate_exp")
        cw_done = sem("cw_done")
        wog_ready = sem("wog_ready")
        ht_high = sem("ht_high")
        ht_low = sem("ht_low")
        raw_in = sem("raw_in")
        b3_added = sem("b3_added")
        w_step = sem("w_step")
        w_split = sem("w_split")
        h_mm = sem("h_mm")
        relu_out = sem("relu_out")
        low_out = sem("low_out")
        l3_mm = sem("l3_mm")
        l3_out = sem("l3_out")
        o_out = [sem(f"o_out{b}") for b in range(B)]

        CONSTS = 6 * 16
        STEPS = HEADROWS * CHUNKS
        QUADS = STILES // 4
        OPS = 4 * TILES
        FLAT = EXPERTS * CHUNKS

        def wait_apart(eng, semaphore, value):
            eng.wait_ge(semaphore, value)
            eng.nop(nofuse=True)

        def on_two(ap, n):
            return ap.unsqueeze(1).to_broadcast([P, n, ap.shape[1]])

        block = ctx.enter_context(nc.Block())

        @block.sync
        def _(sp):
            sp.dma_start(cs[:, :], cols).then_inc(cols_in, 16)
            xv = x.rearrange("b (t p) f -> p b t f", p=P)
            wv = wmod.rearrange("(k p) n -> p k n", p=P)
            for c in range(CHUNKS):
                for b in range(B):
                    t = ds(c * TILES, TILES)
                    sp.dma_start(xs[:, b, t, :], xv[:, b, t, :]).then_inc(x_in[c > 0], 16)
                    if c == 0:
                        n = (slice(0, CHUNK), slice(CHUNK, 3 * CHUNK))[b]
                        sp.dma_start(wm[:, :, n], wv[:, :, n]).then_inc(wmod_in[b], 16)
                if c == 0:
                    sp.dma_start(rs[:, :], rows).then_inc(const_in, 16)
                    sp.dma_start(wqkv[:, :, :], wqkv_t.rearrange("(k p) n -> p k n", p=P)).then_inc(const_in, 16)
                    sp.dma_start(wout[:, :, :], wout_t.rearrange("(k p) n -> p k n", p=P)).then_inc(const_in, 16)
                    sp.dma_start(gatew[:, :, :], gate_t.rearrange("(k p) n -> p k n", p=P)).then_inc(const_in, 16)
                    sp.dma_start(idf[:, :], ident).then_inc(const_in, 16)
                    sp.dma_start(idb[:, :], ident_b).then_inc(const_in, 16)
            def store_parts(c, b):
                sp.wait_ge(parts_ready, c * (4 * B) + 4 * (b + 1))
                for o in range(4):
                    row = (b * KC + o % KC) * P
                    dst = (q_parts, k_parts)[o // KC][:, row:row + P, ds(c * CHUNK, CHUNK)]
                    sp.dma_start(dst.rearrange("r p s -> p r s"), parts[:, b, o]).then_inc(parts_out[b], 16)

            with sp.Fori(0, CHUNKS - 1) as c:
                for b in range(B):
                    store_parts(c, b)

            def load_head(g, s):
                for term, (qr, kr) in enumerate(((0, 0), (0, 1), (0, 2), (1, 0), (1, 1), (2, 0))):
                    for dst, src, r in ((q6, q_parts, qr), (k6, k_parts, kr)):
                        sp.dma_start(dst[term * HD:(term + 1) * HD, s, :],
                                     src[r, ds(g * HD, HD), :]).then_inc(head_in[s], 16)

            def load_m(n, par, s, c):
                sp.wait_ge(mt_copied, n + 1)
                for r in range(PARTS):
                    sp.dma_start(q6[TROWS + r:TROWS + r + 1, s, c * CHUNK:(c + 1) * CHUNK],
                                 mrows[par][r * TILES:(r + 1) * TILES, :]).then_inc(m_in[par], 16)

            store_parts(CHUNKS - 1, 0)
            sp.wait_ge(parts_out[0], 16 * 4 * CHUNKS)
            load_head(0, 0)
            store_parts(CHUNKS - 1, 1)
            sp.wait_ge(parts_out[1], 16 * 4 * CHUNKS)
            load_m(0, 0, 0, 0)

            def steps(i, first, last):
                for s in range(2):
                    if not (last and s == 1):
                        if not (first and s == 0):
                            sp.wait_ge(st_mm, (i * 2 + s) * (CHUNKS * STILES))
                        load_head(i * 2 + (s + 1), 1 - s)
                    for c in range(CHUNKS):
                        if last and s == 1 and c == CHUNKS - 1:
                            continue
                        n = i * (2 * CHUNKS) + (s * CHUNKS + c)
                        load_m(n + 1, (c + 1) % 2, (s + (c + 1) // CHUNKS) % 2, (c + 1) % CHUNKS)

            steps(0, True, False)
            with sp.Fori(1, HEADROWS // 2 - 1) as i:
                steps(i, False, False)
            steps(HEADROWS // 2 - 1, False, True)

            def load_weights(e):
                for l, w in enumerate((w1, w2, w3)):
                    sp.dma_start(raw[:, l], w[e].rearrange("(k p) n -> p k n", p=P)).then_inc(raw_in, 16)
                sp.dma_start(raw_b3[:, :], b3[e]).then_inc(raw_in, 16)

            load_weights(0)
            with sp.Fori(1, EXPERTS) as e:
                wait_apart(sp, w_split, e * 1)
                load_weights(e)
            ov = out.rearrange("b (t p) f -> p b t f", p=P)
            for c in range(CHUNKS):
                for b in range(B):
                    sp.wait_ge(l3_out, 4 * (FLAT - CHUNKS + c + 1) + 2 * (b + 1))
                    t = ds(c * TILES, TILES)
                    sp.dma_start(ov[:, b, t, :], xs[:, b, t, :]).then_inc(o_out[b], 16)
            for b in range(B):
                sp.wait_ge(o_out[b], 16 * CHUNKS)

        @block.tensor
        def _(pe):
            mm = nc.tensor.matmul
            pe.wait_ge(cond_done, 2)
            for n in range(3):
                if n < 2:
                    pe.wait_ge(wmod_in[n], 16)
                for b in range(B):
                    for k in range(KC):
                        last = mm(ps[:, 3 * b + n, :], cond_b[:, k, b, :], wm[:, k, n * CHUNK:(n + 1) * CHUNK],
                                  start=(k == 0), stop=(k == KC - 1))
                if n == 0:
                    last.then_inc(ca_mm, 1)
            for kind, blk in enumerate((SB_, CB)):
                for f in range(KC):
                    for k in range(KC):
                        col = (kind * KC + f) * B
                        last = mm(ps[:, 6, col:col + B], wm[:, k, blk * H + f * P:blk * H + (f + 1) * P],
                                  cond_b[:, k, :, 0], start=(k == 0), stop=(k == KC - 1))
            last.then_inc(mod_mm, 1)

            pe.wait_ge(const_in, CONSTS)
            pe.wait_ge(ca_ready, 1)
            pe.wait_ge(ga_copied, 1)

            def project(c, first):
                for b in range(B):
                    pe.wait_ge(y_ready, c * B + (b + 1))
                    if not (first and b == 0):
                        pe.wait_ge(xn_ready, c * (2 * B) + 2 * b)
                    for k in range(KC):
                        for t in range(TILES):
                            last = nc.tensor.transpose(ps[:, k, t * P:(t + 1) * P],
                                                       y_tile[:, b, t, k * P:(k + 1) * P], idf[:, :])
                    last.then_inc(xt_mm, 1)
                for b in range(B):
                    pe.wait_ge(xn_ready, c * (2 * B) + 2 * (b + 1))
                    for o in range(4):
                        if not (first and b == 0):
                            pe.wait_ge(part1_ready, c * (4 * B) + (4 * b + o - 3))
                        for k in range(KC):
                            last = mm(ps[:, 2 + o, :], wqkv[:, k, o * P:(o + 1) * P], xn_t[:, b, k, :],
                                      start=(k == 0), stop=(k == KC - 1))
                        last.then_inc(qk_mm, 1)
                    for u in range(2):
                        if not (first and b == 0):
                            pe.wait_ge(v_ready, c * (2 * B) + (2 * b + u - 1))
                        for t in (2 * u, 2 * u + 1):
                            for k in range(KC):
                                last = mm(ps[:, 6 + u, (t % 2) * H:(t % 2 + 1) * H],
                                          xn_t[:, b, k, t * P:(t + 1) * P], wqkv[:, k, 2 * H:3 * H],
                                          start=(k == 0), stop=(k == KC - 1))
                        last.then_inc(v_mm, 1)

            project(0, True)
            with pe.Fori(1, CHUNKS) as c:
                project(c, False)

            def scores(n, s, c, u):
                t, kb = u // 4, u % 4
                if not (isinstance(n, int) and n == 0 and u < 3):
                    pe.wait_ge(max_done, n * OPS + (u - BACK[u] + 1))
                q0 = c * CHUNK + t * P
                mm(ps[:, SCORE + RING[u], :], q6[0:TROWS, s, q0:q0 + P],
                   k6[0:TROWS, s, kb * CHUNK:(kb + 1) * CHUNK], start=True, stop=True).then_inc(scores_mm, 1)

            def m_transpose(n, par):
                pe.wait_ge(m_parts, n + 1)
                nc.tensor.transpose(mt_ps, mparts[par][:, :, :].rearrange("p r t -> p (r t)"),
                                    idb[:, :]).then_inc(mt_mm, 1)

            def pv(n, s, q):
                pe.wait_ge(exp_done, n * STILES + 4 * (q + 1))
                if q == 0 and not (isinstance(n, int) and n == 0):
                    pe.wait_ge(acc_out, n)
                for j in range(4):
                    k = 4 * q + j
                    last = mm(ps[32 * j:32 * (j + 1), ACC, :], vs[:, s, k, :], prob[:, k, :],
                              start=(q == 0), stop=(q == QUADS - 1))
                last.then_inc(pv_mm, 1)

            def ctx_out(n, par):
                pe.wait_ge(acc_out, n + 1)
                for t in range(TILES):
                    last = nc.tensor.transpose(ps[:, MISC, t * P:(t + 1) * P], acc_sb[:, par, t * P:(t + 1) * P],
                                               idf[:, :])
                last.then_inc(ctx_mm, 1)

            def steps(i, first, last):
                for s in range(2):
                    for c in range(CHUNKS):
                        n = i * (2 * CHUNKS) + (s * CHUNKS + c)
                        step0 = first and s == 0 and c == 0
                        c2, s2 = (c + 2) % CHUNKS, (s + (c + 2) // CHUNKS) % 2
                        ahead = not (last and s == 1 and c >= 2)
                        if c == 0:
                            pe.wait_ge(v_staged, i * 2 + (s + 1))
                        if c == 2 and ahead:
                            pe.wait_ge(head_in[s2], (i + (s + 1) // 2 + 1) * (HEAD_DMAS * 16))
                        pe.wait_ge(m_in[c % 2], (i * CHUNKS + (s * CHUNKS + c) // 2 + 1) * (PARTS * 16))
                        for q in range(QUADS):
                            for j in range(4):
                                k = 4 * q + j
                                if not (step0 and k < 3):
                                    pe.wait_ge(exp_done, n * STILES + (k - BACK[k] + 1))
                                mm(ps[:, ST + RING[k], :], k6[0:TROWS + PARTS, s, k * P:(k + 1) * P],
                                   q6[0:TROWS + PARTS, s, c * CHUNK:(c + 1) * CHUNK],
                                   start=True, stop=True).then_inc(st_mm, 1)
                                if ahead:
                                    scores(n + 2, s2, c2, k)
                            if q == 0:
                                if not step0:
                                    pv(n - 1, (s + (c - 1) // CHUNKS) % 2, QUADS - 1)
                            else:
                                pv(n, s, q - 1)
                            if q == 1 and not (last and s == 1 and c == CHUNKS - 1):
                                if not (first and s == 0 and c < 2):
                                    pe.wait_ge(ctx_read, n - 1)
                                m_transpose(n + 1, (c + 1) % 2)
                            if q == QUADS - 1 and not step0:
                                if not (last and s == 1 and c == CHUNKS - 1):
                                    pe.wait_ge(mt_copied, n + 2)
                                else:
                                    pe.wait_ge(ctx_read, n - 1)
                                ctx_out(n - 1, (c + 1) % 2)

            pe.wait_ge(fixed_done, 1)
            pe.wait_ge(head_in[0], HEAD_DMAS * 16)
            pe.wait_ge(part1_ready, 4 * B * CHUNKS)
            for n in range(2):
                for u in range(STILES):
                    scores(n, 0, n, u)
                    if n == 1 and u == 5:
                        pe.wait_ge(v_ready, 2 * B * CHUNKS)
                        m_transpose(0, 0)
            pe.wait_ge(mt_copied, 1)
            steps(0, True, False)
            with pe.Fori(1, HEADROWS // 2 - 1) as i:
                steps(i, False, False)
            steps(HEADROWS // 2 - 1, False, True)
            pv(STEPS - 1, 1, QUADS - 1)
            pe.wait_ge(ctx_read, STEPS - 1)
            ctx_out(STEPS - 1, 1)

            def front(c, first):
                for b in range(B):
                    pe.wait_ge(c_copied, c * B + (b + 1))
                    if b == 1 and not (isinstance(c, int) and c < 2):
                        pe.wait_ge(gl_read, c - 1)
                    for k in range(KC):
                        for t in range(TILES):
                            last = nc.tensor.transpose(ps[:, TB[b] + k, t * P:(t + 1) * P],
                                                       c_tile[b][:, t, k * P:(k + 1) * P], idf[:, :])
                    last.then_inc(ct_mm, 1)
                for b in range(B):
                    pe.wait_ge(ct_ready, c * (2 * B) + 2 * (b + 1))
                    if not first:
                        pe.wait_ge(proj_read, c * B + (b - 1))
                    for t in range(TILES):
                        for k in range(KC):
                            last = mm(ps[:, 2 + 2 * b + t // 2, (t % 2) * H:(t % 2 + 1) * H],
                                      ctx_t[b][:, k, t * P:(t + 1) * P], wog[:, b, k, :],
                                      start=(k == 0), stop=(k == KC - 1))
                    last.then_inc(proj_mm, 1)

            def back(c):
                for b in range(B):
                    pe.wait_ge(z_ready, c * B + (b + 1))
                    for k in range(KC):
                        for t in range(TILES):
                            last = nc.tensor.transpose(ps[:, TB[b] + k, t * P:(t + 1) * P],
                                                       z_tile[b][:, t, k * P:(k + 1) * P], idf[:, :])
                    last.then_inc(ht_mm, 1)
                pe.wait_ge(ht_ready, c * (2 * B) + 2 * B)
                for b in range(B):
                    for k in range(KC):
                        n = b * KC + k
                        last = mm(ps[GW * n:GW * (n + 1), 0, :], gatew[:, k, :], hc_t[b][:, k, :],
                                  start=True, stop=True)
                last.then_inc(gate_mm, 1)
                pe.wait_ge(gl_copied, c + 1)
                for t in range(TILES):
                    last = nc.tensor.transpose(ps[:, 7, t * P:(t + 1) * P], gate_sb[:, t * P:(t + 1) * P], idf[:, :])
                last.then_inc(gl_mm, 1)

            pe.wait_ge(wog_ready, B)
            front(0, True)
            front(1, False)
            back(0)
            with pe.Fori(1, CHUNKS - 1) as c:
                front(c + 1, False)
                back(c)
            back(CHUNKS - 1)
            def three(o, stationary, moving):
                n = 0
                for k in range(KC):
                    for a, m in ((0, 0), (1, 0), (0, 1)):
                        last = mm(o, stationary[a](k), moving[m](k), start=(n == 0), stop=(n == 3 * KC - 1))
                        n += 1
                return last

            pe.wait_ge(ht_low, B * KC * CHUNKS)
            with pe.Fori(0, EXPERTS // 2) as e2:
                for s in range(2):
                    wait_apart(pe, w_split, e2 * 2 + (s + 1))
                    with pe.Fori(0, CHUNKS) as c:
                        f = e2 * (2 * CHUNKS) + c + s * CHUNKS
                        for b in range(B):
                            for fo in range(KC):
                                pe.wait_ge(relu_out, f * 8 + (2 * b + fo + 1))
                                three(ps[:, 2 * b + fo, :],
                                      [lambda k, w=w: w[:, s, 0, k, fo * P:(fo + 1) * P] for w in (wx_h, wx_l)],
                                      [lambda k, h=h: h[:, k, b, ds(c * CHUNK, CHUNK)] for h in (ht_h, ht_l)]
                                      ).then_inc(h_mm, 1)
                        for b in range(B):
                            pe.wait_ge(low_out, f * 8 + (2 * b + 4))
                            for fo in range(KC):
                                three(ps[:, 2 * b + fo, :],
                                      [lambda k, w=w: w[:, s, 1, k, fo * P:(fo + 1) * P] for w in (wx_h, wx_l)],
                                      [lambda k, h=h: h[:, 0, b, k, :] for h in (hid_h, hid_l)]).then_inc(h_mm, 1)
                        for b in range(B):
                            pe.wait_ge(low_out, f * 8 + (4 + 2 * b + 4))
                            for u in range(2):
                                pe.wait_ge(l3_out, f * 4 + (2 * b + u + 1))
                                for t in (2 * u, 2 * u + 1):
                                    last = three(ps[:, 4 + 2 * b + u, (t % 2) * H:(t % 2 + 1) * H],
                                                 [lambda k, h=h: h[:, 1, b, k, t * P:(t + 1) * P]
                                                  for h in (hid_h, hid_l)],
                                                 [lambda k, w=w: w[:, s, 2 + b, k, :] for w in (wx_h, wx_l)])
                                last.then_inc(l3_mm, 1)

        @block.scalar
        def _(act):
            act.wait_ge(cols_in, 16)
            nc.scalar.activation(sig, cs[:, C_COND:C_COND + 4], ACT.Exp, scale=-1.0).then_inc(sig_done, 1)
            def leave_psum():
                act.wait_ge(mod_mm, 1)
                for b in range(B):
                    for m, i in ((M_GA, GA), (M_GB, GB)):
                        nc.scalar.activation(mod[:, b, m], ps[:, 3 * b + i // 2, (i % 2) * H:(i % 2 + 1) * H], ACT.Copy)
                cview = ps[:, 6, 0:2 * KC * B].rearrange("p (m k b) -> p m k b", m=2, k=KC)
                nc.scalar.activation(modc[:, :, :, :], cview, ACT.Copy).then_inc(ga_copied, 1)

            def root(nth):
                act.wait_ge(var_ready, nth + 1)
                nc.scalar.activation(std, var, ACT.Sqrt).then_inc(std_ready, 1)

            def first_centred(c):
                act.wait_ge(nmr_ready, c + 1)
                for b in range(B):
                    for t in range(TILES):
                        n = b * TILES + t
                        x_t = xs[:, b, ds(c * TILES + t, 1), :].rearrange("p t f -> p (t f)")
                        last = nc.scalar.activation(h_tile[:, b, t, :], x_t, ACT.Identity,
                                                    scale=rstd[:, n:n + 1], bias=nmr[:, n:n + 1])
                    last.then_inc(ln1_done, 1)

            def transposed(c, b):
                act.wait_ge(xt_mm, c * B + (b + 1))
                for k in range(KC):
                    nc.scalar.activation(xn_t[:, b, k, :], ps[:, k, :], ACT.Identity,
                                         scale=cs[:, C_LNG + k:C_LNG + k + 1],
                                         bias=cs[:, C_LNB + k:C_LNB + k + 1]).then_inc(xn_ready, 1)

            def projected(c, b, o, first):
                act.wait_ge(qk_mm, c * (4 * B) + (4 * b + o + 1))
                if b == 1:
                    act.wait_ge(rest_own, c * 4 + (o + 1))
                elif not first:
                    act.wait_ge(rest_ready, c * 4 + (o - 3))
                bias = cs[:, C_BQK + o:C_BQK + o + 1]
                nc.scalar.activation(qk_f[:, o, :], ps[:, 2 + o, :], ACT.Identity, bias=bias)
                nc.scalar.activation(parts[:, b, o, 0, :], ps[:, 2 + o, :], ACT.Identity,
                                     bias=bias).then_inc(part1_ready, 1)

            def pair(c, first, last):
                transposed(c, 0)
                transposed(c, 1)
                if not last:
                    root(c * 2 + 2)
                    first_centred(c + 1)
                for b in range(B):
                    if not first:
                        act.wait_ge(parts_out[b], c * (16 * 4))
                    for o in range(4):
                        projected(c, b, o, first)
                if not last:
                    root(c * 2 + 3)

            root(0)
            first_centred(0)
            leave_psum()
            root(1)
            pair(0, True, False)
            with act.Fori(1, CHUNKS - 1) as c:
                pair(c, False, False)
            pair(CHUNKS - 1, False, True)

            def acc_copy(n, par):
                act.wait_ge(pv_mm, (n + 1) * QUADS)
                nc.scalar.activation(acc_sb[:, par, :], acc_ps, ACT.Copy).then_inc(acc_out, 1)

            def m_copy(n, par, fresh, in_place):
                if not fresh:
                    act.wait_ge(m_in[par], in_place)
                act.wait_ge(mt_mm, n + 1)
                nc.scalar.activation(mrows[par][:, :], mt_ps, ACT.Copy).then_inc(mt_copied, 1)

            def steps(i, first, last):
                for s in range(2):
                    for c in range(CHUNKS):
                        n = i * (2 * CHUNKS) + (s * CHUNKS + c)
                        step0 = first and s == 0 and c == 0
                        for k in range(STILES):
                            if k % 4 == 0 and not step0:
                                act.wait_ge(pv_mm, (n - 1) * QUADS + (k // 4 + 1))
                            act.wait_ge(st_mm, n * STILES + (k + 1))
                            nc.scalar.activation(prob[:, k, :], ps[:, ST + RING[k], :], ACT.Exp,
                                                 scale=HD ** -0.5).then_inc(exp_done, 1)
                            if k == 4 and not step0:
                                if not (first and s == 0 and c < 3):
                                    act.wait_ge(ctx_mm, n - 2)
                                acc_copy(n - 1, (c + 1) % 2)
                            if k == 9 and not (last and s == 1 and c == CHUNKS - 1):
                                par = (c + 1) % 2
                                m_copy(n + 1, par, step0, (i * CHUNKS + (s * CHUNKS + c + 1 - par) // 2)
                                       * (PARTS * 16))

            for b in range(B):
                act.wait_ge(parts_out[b], 16 * 4 * CHUNKS)
            m_copy(0, 0, True, 0)
            steps(0, True, False)
            with act.Fori(1, HEADROWS // 2 - 1) as i:
                steps(i, False, False)
            steps(HEADROWS // 2 - 1, False, True)
            act.wait_ge(ctx_mm, STEPS - 2)
            acc_copy(STEPS - 1, 1)

            act.wait_ge(ctx_done, STEPS)

            def third_root(c):
                act.wait_ge(var_ready, c + (2 * CHUNKS + 1))
                nc.scalar.activation(std, var, ACT.Sqrt).then_inc(std_ready, 1)

            def front(c):
                for b in range(B):
                    if not (isinstance(c, int) and c == 0):
                        wait_apart(act, ct_mm, (c - 1) * B + (b + 1))
                    nc.scalar.activation(c_tile[b].rearrange("p t (h d) -> p h t d", d=HD),
                                         ctx_h[:, b, :, ds(c * TILES, TILES), :], ACT.Copy).then_inc(c_copied, 1)
                if not isinstance(c, int):
                    third_root(c - 1)
                for b in range(B):
                    act.wait_ge(ct_mm, c * B + (b + 1))
                    if not (isinstance(c, int) and c < 2):
                        act.wait_ge(gate_mm, c - 1)
                        act.wait_ge(ht_low, (c - 2) * (B * KC) + KC * (b + 1))
                    for k in range(KC):
                        nc.scalar.activation(ctx_t[b][:, k, :], ps[:, TB[b] + k, :], ACT.Copy).then_inc(ct_ready, 1)

            def gate_exponent(part):
                act.wait_ge(logits_less, part + 1)
                n = GATE_PARTS[part]
                nc.scalar.activation(gate_p[:, n], gate_p[:, n], ACT.Exp).then_inc(gate_exp, 1)

            def back(c, last=False):
                if isinstance(c, int):
                    third_root(c)
                if last:
                    gate_exponent(0)
                for b in range(B):
                    wait_apart(act, ht_mm, c * B + (b + 1))
                    for k in range(KC):
                        nc.scalar.activation(hc_t[b][:, k, :], ps[:, TB[b] + k, :], ACT.Identity,
                                             bias=modc[:, 0, k, b:b + 1],
                                             scale=modc[:, 1, k, b:b + 1]).then_inc(ht_ready, 1)
                for b in range(B):
                    wait_apart(act, ht_ready, c * (B * KC) + (b + 1) * KC)
                    for k in range(KC):
                        nc.scalar.activation(ht_h[:, k, b, ds(c * CHUNK, CHUNK)], hc_t[b][:, k, :],
                                             ACT.Copy).then_inc(ht_high, 1)
                    if b == 0:
                        wait_apart(act, gate_mm, c + 1)
                        nc.scalar.activation(gate_sb, ps[:, 0, :], ACT.Copy).then_inc(gl_copied, 1)

            act.wait_ge(xr_done, HEADROWS // 2)
            front(0)
            front(1)
            back(0)
            with act.Fori(1, CHUNKS - 1) as c:
                front(c + 1)
                back(c)
            act.wait_ge(ht_low, (CHUNKS - 1) * (B * KC))
            back(CHUNKS - 1, last=True)
            gate_exponent(1)

            with act.Fori(0, EXPERTS // 2) as e2:
                for s in range(2):
                    with act.Fori(0, CHUNKS) as c:
                        f = e2 * (2 * CHUNKS) + c + s * CHUNKS
                        for j in range(8):
                            l, b, fo = j // 4, j // 2 % 2, j % 2
                            bank, bias = ps[:, 2 * b + fo, :], exb[:, s, KC * l + fo:KC * l + fo + 1]
                            act.wait_ge(h_mm, f * 8 + (j + 1))
                            nc.scalar.activation(hid_h[:, l, b, fo, :], bank, ACT.Relu, bias=bias)
                            act.wait_ge(low_out, f * 8 + (j + 1))
                            nc.scalar.activation(h_full[:, j % 2, :], bank, ACT.Relu,
                                                 bias=bias).then_inc(relu_out, 1)

        @block.vector
        def _(dve):
            v = nc.vector
            count = [0]

            def step(ins):
                ins.then_inc(dve_step, 1)
                count[0] += 1
                dve.wait_ge(dve_step, count[0])

            dve.wait_ge(cols_in, 16)
            dve.wait_ge(sig_done, 1)
            step(v.tensor_scalar(mneg, sig, 1.0, None, ALU.add))
            step(v.reciprocal(mres, mneg))
            step(v.tensor_tensor(silu, mres, cs[:, C_COND:C_COND + 4], ALU.mult))
            for k in range(KC):
                v.tensor_copy(cond_b[:, k], silu[:, k * B:(k + 1) * B].unsqueeze(2).to_broadcast([P, B, P])
                              ).then_inc(cond_done, 1)
            LN = 7

            def normalise(src, at, nth, between=None):
                for b in range(B):
                    for t in range(TILES):
                        last = v.bn_stats(stats[:, b * TILES + t, :], src(b, t))
                last.then_inc(dve_step, 1)
                if between:
                    at += between(at + 1)
                wait_apart(dve, dve_step, at + 1)
                for t in range(B * TILES):
                    last = v.bn_aggr(mv[:, t, :], stats[:, t, :])
                last.then_inc(dve_step, 1)
                dve.wait_ge(dve_step, at + 2)
                v.tensor_scalar(var, mv[:, :, 1], EPS, None, ALU.add).then_inc(var_ready, 1)
                dve.wait_ge(std_ready, nth + 1)
                v.reciprocal(rstd, std).then_inc(dve_step, 1)
                dve.wait_ge(dve_step, at + 3)
                v.tensor_tensor(std, rstd, rstd, ALU.mult).then_inc(dve_step, 1)
                dve.wait_ge(dve_step, at + 4)
                v.tensor_tensor(std, std, var, ALU.mult).then_inc(dve_step, 1)
                dve.wait_ge(dve_step, at + 5)
                v.tensor_scalar(std, std, -0.5, 1.5, ALU.mult, ALU.add).then_inc(dve_step, 1)
                dve.wait_ge(dve_step, at + 6)
                v.tensor_tensor(rstd, rstd, std, ALU.mult).then_inc(dve_step, 1)
                dve.wait_ge(dve_step, at + 7)

            def centred(dst, src, b, t):
                return v.tensor_scalar(dst, src, mv[:, b * TILES + t, 0:1],
                                       rstd[:, b * TILES + t:b * TILES + t + 1], ALU.subtract, ALU.mult)

            def x_tile(b, t):
                return xs[:, b, ds(t, 1), :].rearrange("p t f -> p (t f)")

            def first_norm(c, at):
                normalise(lambda b, t: x_tile(b, c * TILES + t), at, c * 2)
                v.scalar_tensor_tensor(nmr, mv[:, :, 0], -1.0, rstd, ALU.mult, ALU.mult).then_inc(nmr_ready, 1)
                v.tensor_copy(mean1[:, :, ds(c * TILES, TILES)], mv[:, :, 0].rearrange("p (b t) -> p b t", b=B))
                v.tensor_copy(rstd1[:, :, ds(c * TILES, TILES)], rstd.rearrange("p (b t) -> p b t", b=B))

            def second_norm(c, at):
                def h_of(b, t):
                    if t == 0:
                        if not (isinstance(c, int) and c == 0):
                            wait_apart(dve, h_ready, c * B + (b + 1 - B))
                    return h_tile[:, b, t, :]

                normalise(h_of, at, c * 2 + 1)
                for b in range(B):
                    for t in range(TILES):
                        last = centred(y_tile[:, b, t, :], h_tile[:, b, t, :], b, t)
                    last.then_inc(y_ready, 1)

            def split(c, b, at, first=False):
                for o in range(4):
                    if b == 0:
                        left = rest_v
                        if not (first and o == 0):
                            wait_apart(dve, parts_ready, c * (4 * B) + o)
                        dve.wait_ge(part1_ready, c * (4 * B) + (o + 1))
                        v.tensor_tensor(left, qk_f[:, o, :], parts[:, b, o, 0, :], ALU.subtract).then_inc(rest_own, 1)
                        dve.wait_ge(rest_own, c * 4 + (o + 1))
                    else:
                        left = rest[o]
                        dve.wait_ge(rest_ready, c * 4 + (o + 1))
                    v.tensor_copy(parts[:, b, o, 1, :], left).then_inc(dve_step, 1)
                    dve.wait_ge(dve_step, at + o + 1)
                    v.tensor_tensor(parts[:, b, o, 2, :], left, parts[:, b, o, 1, :],
                                    ALU.subtract).then_inc(parts_ready, 1)
                for u in range(2):
                    dve.wait_ge(v_mm, c * (2 * B) + (2 * b + u + 1))
                    v.tensor_tensor(
                        v_heads[:, b * HEADS:(b + 1) * HEADS, ds(c * TILES + 2 * u, 2), :].rearrange(
                            "p h t d -> p t h d"),
                        ps[:, 6 + u, :].rearrange("p (t h d) -> p t h d", t=2, d=HD),
                        on_two(rs[:, R_BV:R_BV + H], 2).rearrange("p t (h d) -> p t h d", d=HD),
                        ALU.add).then_inc(v_ready, 1)

            NORMS, SPLITS = 2 * LN, B * 4

            def pair(c, at, first):
                first_norm(c + 1, at)
                at += LN
                if not first:
                    split(c - 1, 1, at)
                    at += 4
                split(c, 0, at, first)
                second_norm(c + 1, at + 4)

            dve.wait_ge(x_in[0], 16 * B)
            base = count[0]
            first_norm(0, base)
            count[0] = base + LN
            dve.wait_ge(ca_mm, 1)
            for b in range(B):
                def blk(i):
                    return ps[:, 3 * b + i // 2, (i % 2) * H:(i % 2 + 1) * H]
                v.tensor_scalar(mod[:, b, M_CA], blk(CA), 1.0, None, ALU.add)
                last = v.tensor_copy(mod[:, b, M_SA], blk(SA))
            last.then_inc(ca_ready, 1)
            dve.wait_ge(ca_ready, 1)
            for b in range(B):
                dve.wait_ge(ln1_done, b + 1)
                h = h_tile[:, b]
                step(v.tensor_tensor(h, h, on_two(mod[:, b, M_CA], TILES), ALU.mult))
                v.tensor_tensor(h, h, on_two(mod[:, b, M_SA], TILES), ALU.add).then_inc(h_first, 1)
            dve.wait_ge(h_first, B)

            base = count[0]
            second_norm(0, base)
            base += LN
            dve.wait_ge(x_in[1], 16 * B * (CHUNKS - 1))
            dve.wait_ge(const_in, CONSTS)
            pair(0, base, True)
            base += NORMS + 4
            with dve.Fori(1, CHUNKS - 1) as c:
                pair(c, c * (NORMS + SPLITS) + (base - (NORMS + SPLITS)), False)
            base += (NORMS + SPLITS) * (CHUNKS - 2)
            split(CHUNKS - 2, 1, base)
            split(CHUNKS - 1, 0, base + 4)
            base += SPLITS
            dve.wait_ge(ga_copied, 1)
            count[0] = base
            v.tensor_scalar(modc[:, 1], modc[:, 1], 1.0, None, ALU.add)
            for b in range(B):
                g2 = mod[:, b, M_GA:M_GB + 1].rearrange("p m f -> p (m f)")
                v.tensor_scalar(gtmp[:, 0], g2, 0.0, 2.0, ALU.is_ge, ALU.mult)
                step(v.tensor_scalar(gtmp[:, 1], g2, -1.0, FLOOR, ALU.mult, ALU.max))
                step(v.tensor_tensor(gtmp[:, 1], g2, gtmp[:, 1], ALU.max))
                step(v.scalar_tensor_tensor(g2, gtmp[:, 0], -1.0, gtmp[:, 1], ALU.add, ALU.mult))
                v.tensor_tensor(gah[:, b, 0], mod[:, b, M_GA], mod[:, b, M_CA], ALU.mult)
                step(v.tensor_tensor(gtmp[:, 0, 0:H], mod[:, b, M_SA], rs[:, R_BO:R_BO + H], ALU.add))
                v.tensor_tensor(gah[:, b, 1], gtmp[:, 0, 0:H], mod[:, b, M_GA], ALU.mult).then_inc(gates_done, 1)
                dve.wait_ge(gates_done, b + 1)
            base = count[0]
            split(CHUNKS - 1, 1, base)
            base += 4

            def maximum(n, par, o):
                dve.wait_ge(scores_mm, n * OPS + (o + 1))
                if o == 0 and not (isinstance(n, int) and n < 2):
                    dve.wait_ge(top_done, n - 1)
                v.tensor_reduce(mx[par][:, o // 4, o % 4:o % 4 + 1], ps[:, SCORE + RING[o], :],
                                AX.X, ALU.max).then_inc(max_done, 1)

            def top(n, par, fresh):
                dve.wait_ge(max_done, (n + 1) * OPS)
                if not fresh:
                    dve.wait_ge(m_parts, n - 1)
                v.tensor_reduce(mtop[par], mx[par], AX.X, ALU.max).then_inc(top_done, 1)

            def context_sum(n, par):
                dve.wait_ge(ctx_mm, n + 1)
                if not (isinstance(n, int) and n < 2):
                    dve.wait_ge(ctx_done, n - 1)
                v.tensor_reduce(ctx_sum[par], ctx_ps[:, :, :, 0:HD + 1].rearrange("p t g n -> p t n g"),
                                AX.X, ALU.add).then_inc(ctx_read, 1)

            def context_rec(n, par):
                dve.wait_ge(ctx_read, n + 1)
                v.reciprocal(rec[par], ctx_sum[par][:, :, HD]).then_inc(rec_ready, 1)

            def steps(i, first, last):
                for s in range(2):
                    for c in range(CHUNKS):
                        n = i * (2 * CHUNKS) + (s * CHUNKS + c)
                        for o in range(OPS):
                            if not (last and s == 1 and c >= 2):
                                maximum(n + 2, c % 2, o)
                            if o == 1 and not (last and s == 1 and c == CHUNKS - 1):
                                top(n + 1, (c + 1) % 2, first and s == 0 and c == 0)
                            if not (first and s == 0 and c < 2):
                                if o == 3:
                                    context_sum(n - 2, c % 2)
                                elif o == 5:
                                    context_rec(n - 2, c % 2)

            for n in range(2):
                for o in range(OPS):
                    maximum(n, n, o)
                if n == 0:
                    top(0, 0, True)
            steps(0, True, False)
            with dve.Fori(1, HEADROWS // 2 - 1) as i:
                steps(i, False, False)
            steps(HEADROWS // 2 - 1, False, True)
            for n in (STEPS - 2, STEPS - 1):
                context_sum(n, n % 2)
                context_rec(n, n % 2)

            def proj_add(c, at, between=None):
                for b in range(B):
                    dve.wait_ge(proj_mm, c * B + (b + 1))
                    for u in range(2):
                        xt = xs[:, b, ds(c * TILES + 2 * u, 2), :]
                        last = v.tensor_tensor(xt, xt, ps[:, 2 + 2 * b + u, :].rearrange("p (t f) -> p t f", f=H),
                                               ALU.add)
                    last.then_inc(proj_read, 1)
                wait_apart(dve, proj_read, c * B + B)
                normalise(lambda b, t: x_tile(b, c * TILES + t), at, c + 2 * CHUNKS, between)
                for b in range(B):
                    for t in range(TILES):
                        last = centred(z_tile[b][:, t, :], x_tile(b, c * TILES + t), b, t)
                    last.then_inc(z_ready, 1)

            def gate_logits(c):
                dve.wait_ge(gl_mm, c + 1)
                l = logits[:, ds(c * TILES, TILES), :, :]
                v.tensor_reduce(l, gl_ps[:, :, :, :, 0:EXPERTS].rearrange("p t b k e -> p t b e k"), AX.X,
                                ALU.add).then_inc(gl_summed, 1)
                wait_apart(dve, gl_summed, c + 1)
                l = l.rearrange("p t b e -> p (t b) e")
                v.tensor_tensor(l, l, on_two(rs[:, R_GB:R_GB + EXPERTS], TILES * B), ALU.add).then_inc(gl_read, 1)

            left, where, one, two = gate_wide
            highest, at_highest, total, inv = gate_slim

            def over(a):
                return a.unsqueeze(2).to_broadcast([P, a.shape[1], EXPERTS])

            def gate_less(part):
                n = GATE_PARTS[part]
                step(v.tensor_reduce(highest[:, n], gate_p[:, n], AX.X, ALU.max))
                v.tensor_tensor(gate_p[:, n], gate_p[:, n], over(highest[:, n]), ALU.subtract).then_inc(logits_less, 1)

            def gate_choose(part):
                n = GATE_PARTS[part]
                g_, l_, w_, o_, t_ = (a[:, n] for a in (gate_p, left, where, one, two))
                iota = on_two(cs[:, C_IOTA:C_IOTA + EXPERTS], n.stop - n.start)
                dve.wait_ge(gate_exp, part + 1)
                step(v.tensor_reduce(total[:, n], g_, AX.X, ALU.add))
                step(v.reciprocal(inv[:, n], total[:, n]))
                step(v.tensor_tensor(l_, g_, over(inv[:, n]), ALU.mult))
                step(v.tensor_copy(g_, l_))
                for chosen in (o_, t_):
                    step(v.tensor_reduce(highest[:, n], l_, AX.X, ALU.max))
                    step(v.tensor_tensor(w_, l_, over(highest[:, n]), ALU.is_lt))
                    step(v.scalar_tensor_tensor(w_, w_, float(EXPERTS), iota, ALU.mult, ALU.add))
                    step(v.tensor_reduce(at_highest[:, n], w_, AX.X, ALU.min))
                    step(v.tensor_tensor(chosen, iota, over(at_highest[:, n]), ALU.is_equal))
                    if chosen is o_:
                        step(v.scalar_tensor_tensor(l_, o_, -2.0, l_, ALU.mult, ALU.add))
                wide = [P, n.stop - n.start, EXPERTS]
                v.tensor_tensor(o_, o_, g_[:, :, 0:1].to_broadcast(wide), ALU.mult)
                step(v.tensor_tensor(t_, t_, g_[:, :, 1:2].to_broadcast(wide), ALU.mult))
                v.tensor_tensor(gate_w[:, n], o_, t_, ALU.add).then_inc(cw_done, 1)

            proj_add(0, base)
            with dve.Fori(1, CHUNKS - 1) as c:
                def logits_before(at):
                    gate_logits(c - 1)
                    wait_apart(dve, ht_mm, c * B)
                    return 0

                proj_add(c, c * LN + base, logits_before)

            def less_before(at):
                gate_logits(CHUNKS - 2)
                dve.wait_ge(gl_read, CHUNKS - 1)
                dve.wait_ge(ct_mm, B * CHUNKS)
                count[0] = at
                gate_less(0)
                dve.wait_ge(ht_mm, (CHUNKS - 1) * B)
                return 1

            base += LN * (CHUNKS - 1)
            proj_add(CHUNKS - 1, base, less_before)
            count[0] = base + LN + 1
            gate_choose(0)
            gate_logits(CHUNKS - 1)
            dve.wait_ge(gl_read, CHUNKS)
            v.memset(free_at_first[:, 0:1], 0.0).then_inc(relu_out, 4)
            v.memset(free_at_first[:, 1:2], 0.0).then_inc(l3_out, 4)
            v.memset(free_at_first[:, 2:3], 0.0).then_inc(low_out, 2)
            gate_less(1)
            gate_choose(1)
            dve.wait_ge(cw_done, 2)

            with dve.Fori(0, EXPERTS // 2) as e2:
                for s in range(2):
                    with dve.Fori(0, CHUNKS) as c:
                        f = e2 * (2 * CHUNKS) + c + s * CHUNKS
                        def add(b, t, value):
                            tile = xs[:, b, ds(c * TILES + t, 1), :].rearrange("p t f -> p (t f)")
                            w = cw[:, ds(c * TILES + t, 1), b, ds(e2 * 2 + s, 1)].rearrange("p t e -> p (t e)")
                            return v.scalar_tensor_tensor(tile, value, w, tile, ALU.mult, ALU.add)

                        for j in range(8):
                            l, b, fo = j // 4, j // 2 % 2, j % 2
                            dve.wait_ge(relu_out, f * 8 + (4 + j + 1))
                            v.tensor_tensor(hid_l[:, l, b, fo, :], h_full[:, j % 2, :],
                                            hid_h[:, l, b, fo, :].bitcast(f32), ALU.subtract).then_inc(low_out, 1)
                            last = add(j // TILES, j % TILES, b3x[s][:, j // TILES])
                        last.then_inc(b3_added, 1)
                        wait_apart(dve, b3_added, f + 1)
                        for b in range(B):
                            for u in range(2):
                                dve.wait_ge(l3_mm, f * 4 + (2 * b + u + 1))
                                for t in (2 * u, 2 * u + 1):
                                    last = add(b, t, ps[:, 4 + 2 * b + u, (t % 2) * H:(t % 2 + 1) * H])
                                last.then_inc(l3_out, 1)

        @block.gpsimd
        def _(pool):
            g = nc.gpsimd
            g.memset(vs[:, :, :, HD + 1:VW], 0.0)
            g.memset(vs[:, :, :, HD:HD + 1], 1.0).then_inc(fills, 1)
            pool.wait_ge(fills, 1)
            g.memset(k6[96:128, :, :], 1.0).then_inc(fixed_done, 1)
            pool.wait_ge(fixed_done, 1)
            pool.wait_ge(ca_ready, 1)
            def modulate(c, b, at):
                h = h_tile[:, b]
                pool.wait_ge(ln1_done, c * B + (b + 1))
                g.tensor_tensor(h, h, on_two(mod[:, b, M_CA], TILES), ALU.mult).then_inc(pool_step, 1)
                pool.wait_ge(pool_step, at)
                g.tensor_tensor(h, h, on_two(mod[:, b, M_SA], TILES), ALU.add).then_inc(h_ready, 1)

            def leave(c, o, first):
                if not first:
                    pool.wait_ge(parts_ready, c * (4 * B) + (o + 1 - 4 * B + 4))
                pool.wait_ge(part1_ready, c * (4 * B) + (4 + o + 1))
                g.tensor_tensor(rest[o], qk_f[:, o, :], parts[:, 1, o, 0, :], ALU.subtract).then_inc(rest_ready, 1)

            def pair(c, first, last):
                if not last:
                    for b in range(B):
                        modulate(c + 1, b, c * B + (b + 1))
                for o in range(4):
                    leave(c, o, first)

            pair(0, True, False)
            with pool.Fori(1, CHUNKS - 1) as c:
                pair(c, False, False)
            pair(CHUNKS - 1, False, True)
            base = B * (CHUNKS - 1)

            def stage_v(gi, s):
                g.tensor_copy(vs[:, s, :, 0:HD], v_heads[:, ds(gi, 1), :, :].rearrange(
                    "p g t d -> p (g t) d")).then_inc(v_staged, 1)

            def residual(i):
                for b in range(B):
                    x_t = xs[:, b, ds(i * 1, 1), :].rearrange("p t f -> p (t f)")
                    r = xr[:, b]
                    wide = [P, H]
                    chain = ((r, x_t, mean1[:, b, ds(i * 1, 1)].to_broadcast(wide), ALU.subtract),
                             (r, r, rstd1[:, b, ds(i * 1, 1)].to_broadcast(wide), ALU.mult),
                             (r, r, gah[:, b, 0], ALU.mult), (r, r, gah[:, b, 1], ALU.add))
                    for n, (o, a0, a1, op) in enumerate(chain):
                        g.tensor_tensor(o, a0, a1, op).then_inc(xr_step, 1)
                        wait_apart(pool, xr_step, i * (4 * B) + (4 * b + n + 1))
                    ins = g.tensor_tensor(x_t, x_t, r, ALU.add)
                ins.then_inc(xr_done, 1)

            STEP = 5

            def m_prepare(n, par, fresh):
                at = n * STEP + base
                if not fresh:
                    pool.wait_ge(mt_mm, n - 1)
                wait_apart(pool, top_done, n + 1)
                pa = mparts[par]
                g.tensor_scalar(mneg, mtop[par], -1.0, None, ALU.mult).then_inc(pool_step, 1)
                wait_apart(pool, pool_step, at + 1)
                g.tensor_copy(pa[:, 0, :], mneg).then_inc(pool_step, 1)
                pool.wait_ge(pool_step, at + 2)
                g.tensor_tensor(mres, mneg, pa[:, 0, :], ALU.subtract).then_inc(pool_step, 1)
                wait_apart(pool, pool_step, at + 3)
                g.tensor_copy(pa[:, 1, :], mres).then_inc(pool_step, 1)
                pool.wait_ge(pool_step, at + 4)
                g.tensor_tensor(mres2, mres, pa[:, 1, :], ALU.subtract).then_inc(pool_step, 1)
                wait_apart(pool, pool_step, at + 5)
                g.tensor_copy(pa[:, 2, :], mres2).then_inc(m_parts, 1)

            def context(n, par):
                wait_apart(pool, rec_ready, n + 1)
                g.tensor_tensor(ctx_q[:, ds(n * TILES, TILES), :], ctx_sum[par][:, :, 0:HD],
                                rec[par].unsqueeze(2).to_broadcast([P, TILES, HD]),
                                ALU.mult).then_inc(ctx_done, 1)

            def steps(i, first, last):
                for s in range(2):
                    for c in range(CHUNKS):
                        n = i * (2 * CHUNKS) + (s * CHUNKS + c)
                        if c == 1 and not (last and s == 1):
                            if not (first and s == 0):
                                wait_apart(pool, pv_mm, (i * 2 + s) * (CHUNKS * QUADS))
                            stage_v(i * 2 + (s + 1), 1 - s)
                        if not (last and s == 1 and c == CHUNKS - 1):
                            m_prepare(n + 1, (c + 1) % 2, first and s == 0 and c == 0)
                        if not (first and s == 0 and c < 2):
                            context(n - 2, c % 2)
                        if s == 0 and c == 2:
                            residual(i)

            pool.wait_ge(v_ready, 2 * B * CHUNKS)
            pool.wait_ge(fixed_done, 1)
            stage_v(0, 0)
            m_prepare(0, 0, True)
            pool.wait_ge(gates_done, B)
            for b in range(B):
                g.tensor_tensor(wog[:, b], wout[:, :, :], on_two(mod[:, b, M_GA], KC), ALU.mult).then_inc(wog_ready, 1)
            steps(0, True, False)
            with pool.Fori(1, HEADROWS // 2 - 1) as i:
                steps(i, False, False)
            steps(HEADROWS // 2 - 1, False, True)
            for n in (STEPS - 2, STEPS - 1):
                context(n, n % 2)

            def split_expert(e, s, at):
                if not (isinstance(e, int) and e < 2):
                    wait_apart(pool, l3_out, (e - 1) * (4 * CHUNKS) + 4)
                wait_apart(pool, raw_in, (e + 1) * (4 * 16))
                for b in range(B):
                    g.tensor_tensor(b3x[s][:, b], raw_b3[:, :], mod[:, b, M_GB], ALU.mult)
                g.tensor_copy(exb[:, s, :], cs[:, ds(C_EB + e * (2 * KC), 2 * KC)])
                n = 0
                for slot in range(2):
                    g.tensor_copy(wx_h[:, s, slot], raw[:, slot]).then_inc(w_step, 1)
                    wait_apart(pool, w_step, at + (n + 1))
                    g.tensor_tensor(wx_l[:, s, slot], raw[:, slot], wx_h[:, s, slot].bitcast(f32),
                                    ALU.subtract).then_inc(w_step, 1)
                    n += 2
                for b in range(B):
                    pool.wait_ge(w_step, at + n)
                    g.tensor_tensor(w3g, raw[:, 2], on_two(mod[:, b, M_GB], KC), ALU.mult).then_inc(w_step, 1)
                    wait_apart(pool, w_step, at + (n + 1))
                    g.tensor_copy(wx_h[:, s, 2 + b], w3g).then_inc(w_step, 1)
                    pool.wait_ge(w_step, at + (n + 2))
                    g.tensor_tensor(wx_l[:, s, 2 + b], w3g, wx_h[:, s, 2 + b].bitcast(f32),
                                    ALU.subtract).then_inc(w_split if b else w_step, 1)
                    n += 3

            PER = 9
            def low(c):
                for b in range(B):
                    for k in range(KC):
                        pool.wait_ge(ht_high, c * (B * KC) + (b * KC + k + 1))
                        t = ds(c * CHUNK, CHUNK)
                        g.tensor_tensor(ht_l[:, k, b, t], hc_t[b][:, k, :], ht_h[:, k, b, t].bitcast(f32),
                                        ALU.subtract).then_inc(ht_low, 1)

            pool.wait_ge(ctx_done, STEPS)
            split_expert(0, 0, 0)
            with pool.Fori(0, CHUNKS) as c:
                low(c)
            pool.wait_ge(proj_mm, B * CHUNKS)
            pool.wait_ge(cw_done, 2)
            split_expert(1, 1, PER)
            with pool.Fori(1, EXPERTS // 2) as e2:
                for s in range(2):
                    split_expert(e2 * 2 + s, s, e2 * (2 * PER) + s * PER)


def kernel(**inputs):
    import ml_dtypes
    import numpy as np
    from concourse import bacc
    from concourse.bass_utils import run_bass_kernel_spmd

    a = {n.replace("L0_", ""): np.asarray(v) for n, v in inputs.items()}

    def columns(v):
        return v.reshape(-1, KC, P).transpose(2, 0, 1).reshape(P, -1)

    def repeated(v):
        return np.broadcast_to(v.reshape(1, -1), (P, v.size))

    cond = a["c"].reshape(B, KC, P).transpose(2, 1, 0).reshape(P, KC * B)
    cols = np.concatenate([cond, columns(a["attn_b_qkv"][:2 * H]), columns(a["attn_ln_gamma"]),
                           columns(a["attn_ln_beta"]), columns(np.stack([a["ffn_b1"], a["ffn_b2"]], axis=1)),
                           repeated(np.arange(EXPERTS, dtype=np.float32))], axis=1)
    rows = np.concatenate([repeated(a["attn_b_qkv"][2 * H:]), repeated(a["attn_b_out"]),
                           repeated(a["ffn_gate_b"])], axis=1)
    eye = np.eye(P, dtype=np.float32)
    arrays = {
        "x": a["attn_hidden_states"], "cols": cols, "rows": rows, "wmod": a["wmod"],
        "wqkv_t": a["attn_W_qkv"].T, "wout_t": a["attn_W_out"].T,
        "gate_t": np.pad(a["ffn_gate_w"].T, ((0, 0), (0, GW - EXPERTS))),
        "w1": a["ffn_w1"], "w2": a["ffn_w2"], "w3": a["ffn_w3"],
        "b3": np.broadcast_to(a["ffn_b3"][:, None, :], (EXPERTS, P, H)),
        "ident": eye, "ident_b": eye.astype(ml_dtypes.bfloat16),
    }
    arrays = {n: np.ascontiguousarray(v) for n, v in arrays.items()}
    nc = bacc.Bacc("TRN2", target_bir_lowering=False, num_devices=1)
    aps = {n: nc.dram_tensor(n, v.shape, mybir.dt.from_np(v.dtype), kind="ExternalInput").ap()
           for n, v in arrays.items()}
    out = nc.dram_tensor("out", (B, S, H), mybir.dt.float32, kind="ExternalOutput").ap()
    build(nc, out=out, **aps)
    return run_bass_kernel_spmd(nc, [arrays], core_ids=[0]).results[0]["out"]
```
